# Optimizing a Trainium2 kernel written in Bass

```python
import numpy as np
import jax
import jax.numpy as jnp

def _softmax(x, axis=-1):
    return jax.nn.softmax(x, axis=axis)

def _gelu(x):
    return jax.nn.gelu(x, approximate=True)

def _silu(x):
    return jax.nn.silu(x)

def _sigmoid(x):
    return jax.nn.sigmoid(x)

def _layernorm(x, axis=-1, eps=1e-05):
    m = jnp.mean(x, axis=axis, keepdims=True)
    v = jnp.var(x, axis=axis, keepdims=True)
    return (x - m) / jnp.sqrt(v + eps)

def _scatter_add(tgt, idx, src, axis=0):
    return tgt.at[idx].add(src)

def _segment_sum(src, seg, n):
    return jax.ops.segment_sum(src, seg, n)
kernel_name = 'mk_flamingo_gated_d4_seqx_r8_818766'

def setup_inputs(seed: int=0):
    np.random.seed(seed)
    _w = jnp.asarray

    def _rec_inputs():
        import jax
        import jax.numpy as jnp
        _rk = jax.random.key(seed)
        x = -0.0003929 + 0.9999 * jax.random.normal(jax.random.fold_in(_rk, 1), (2, 256, 512), jnp.float32)
        _lenS = 256 - jax.random.randint(jax.random.fold_in(_rk, 7), (2,), 0, max(1, 256 // 4) + 1, jnp.int32)
        _lenS2 = 512 - jax.random.randint(jax.random.fold_in(_rk, 8), (2,), 0, max(1, 512 // 4) + 1, jnp.int32)
        _ctx_4096P = jax.random.normal(jax.random.fold_in(_rk, 11), (2, 16, 512), jnp.float32)
        _ctx_4096c = jax.random.dirichlet(jax.random.fold_in(_rk, 511), 0.3 * jnp.ones((16,), jnp.float32), (2, 512))
        _ctx_4096t = jnp.einsum('bsk,bkd->bsd', _ctx_4096c, _ctx_4096P)
        _ctx_4096t = _ctx_4096t * jax.lax.rsqrt(jnp.mean(jnp.square(_ctx_4096t)) + 1e-12) * 0.953939
        ctx_4096 = 2.81802e-05 + 1.00001 * (_ctx_4096t + 0.3 * jax.random.normal(jax.random.fold_in(_rk, 611), (2, 512, 512), jnp.float32))
        _validS = jnp.arange(256)[None, :] < _lenS[:, None]
        _validS2 = jnp.arange(512)[None, :] < _lenS2[:, None]
        _causal = jnp.tril(jnp.ones((256, 256), dtype=bool))
        mask_1x1xSxS2_ff0 = jnp.where(jnp.ones((1, 1, 256, 512), dtype=bool), 0.0, -1000000000.0).astype(jnp.float32)
        _g = jax.random.normal(jax.random.fold_in(_rk, 9001), (2, 4), jnp.float32)
        _g = jnp.sign(_g) * jnp.maximum(jnp.abs(_g), 1.0) + (_g == 0) * 1.0
        g_xattn = _g[0]
        g_ffn = _g[1]
        return (x, ctx_4096, mask_1x1xSxS2_ff0, g_xattn, g_ffn)
    x, ctx_4096, mask_1x1xSxS2_ff0, g_xattn, g_ffn = _rec_inputs()

    def _L0_xattn_setup():
        import jax, jax.numpy as jnp
        import numpy as np
        HID = 512
        NHEAD = 32
        NKV = 8
        HDIM = 128
        G = NHEAD // NKV
        key = jax.random.key(seed)
        ks = jax.random.split(key, 6)
        s = 0.02
        B, L = (2, 256)
        return {'query': jax.random.normal(ks[0], (B, L, HID), jnp.float32), 'kv': jax.random.normal(ks[1], (B, L, HID), jnp.float32), 'Wq': jax.random.normal(ks[2], (HID, NHEAD * HDIM), jnp.float32) * s, 'bq': jnp.zeros((NHEAD * HDIM,), jnp.float32), 'Wkv': jax.random.normal(ks[3], (HID, 2 * NKV * HDIM), jnp.float32) * s, 'bkv': jnp.zeros((2 * NKV * HDIM,), jnp.float32), 'Wo': jax.random.normal(ks[4], (NHEAD * HDIM, HID), jnp.float32) * s, 'bo': jnp.zeros((HID,), jnp.float32)}
    _L0_xattn_all = _L0_xattn_setup()
    _L0_xattn_in = {k: v for k, v in _L0_xattn_all.items() if k in ('Wq', 'bq', 'Wkv', 'bkv', 'Wo', 'bo')}
    del _L0_xattn_all

    def _L0_ffn_setup():
        import jax, jax.numpy as jnp
        import numpy as np
        B, S, DIN, DOUT = (8, 256, 512, 512)
        THRESH = 0.1
        LN_EPS = 1e-05
        key = jax.random.key(seed)
        k_x, k_w = jax.random.split(key)
        x = jax.random.normal(k_x, (B, S, DIN), dtype=jnp.float32)
        weight = (jax.random.uniform(k_w, (DOUT, DIN), dtype=jnp.float32) - 0.5) * 0.2
        bias = jnp.zeros((DOUT,), dtype=jnp.float32)
        scale = jnp.ones((DOUT,), dtype=jnp.float32)
        ln_gamma = jnp.ones((DOUT,), dtype=jnp.float32)
        ln_beta = jnp.zeros((DOUT,), dtype=jnp.float32)
        quant_scale = jnp.ones((1,), dtype=jnp.float32) * 10.0
        return {'x': x, 'weight': weight, 'bias': bias, 'scale': scale, 'ln_gamma': ln_gamma, 'ln_beta': ln_beta, 'quant_scale': quant_scale}
    _L0_ffn_all = _L0_ffn_setup()
    _L0_ffn_in = {k: v for k, v in _L0_ffn_all.items() if k in ('weight', 'bias', 'scale', 'ln_gamma', 'ln_beta', 'quant_scale')}
    del _L0_ffn_all

    def _L1_xattn_setup():
        import jax, jax.numpy as jnp
        import numpy as np
        EMB_DIM = 512
        NHEADS = 32
        KVHEADS = 8
        HEAD_DIM = 128
        ROPE_BASE = 10000.0

        def _rope(x):
            B, H, S, D = x.shape
            inv_freq = 1.0 / ROPE_BASE ** (jnp.arange(0, D, 2, dtype=jnp.float32) / D)
            ang = jnp.arange(S, dtype=jnp.float32)[:, None] * inv_freq[None, :]
            cos = jnp.concatenate([jnp.cos(ang), jnp.cos(ang)], axis=-1)
            sin = jnp.concatenate([jnp.sin(ang), jnp.sin(ang)], axis=-1)
            x1, x2 = (x[..., :D // 2], x[..., D // 2:])
            rot = jnp.concatenate([-x2, x1], axis=-1)
            return x * cos + rot * sin
        key = jax.random.key(seed)
        ks = jax.random.split(key, 7)
        B, S = (2, 256)
        std_qk = EMB_DIM ** (-0.5)
        std_vd = (1.0 / (EMB_DIM * NHEADS * HEAD_DIM) ** 0.5) ** 0.5
        return {'q': jax.random.normal(ks[0], (B, S, EMB_DIM), jnp.float32), 'k': jax.random.normal(ks[1], (B, S, EMB_DIM), jnp.float32), 'v': jax.random.normal(ks[2], (B, S, EMB_DIM), jnp.float32), 'Wq': jax.random.normal(ks[3], (NHEADS * HEAD_DIM, EMB_DIM), jnp.float32) * std_qk, 'Wk': jax.random.normal(ks[4], (KVHEADS * HEAD_DIM, EMB_DIM), jnp.float32) * std_qk, 'Wv': jax.random.normal(ks[5], (KVHEADS * HEAD_DIM, EMB_DIM), jnp.float32) * std_vd, 'Wd': jax.random.normal(ks[6], (EMB_DIM, NHEADS * HEAD_DIM), jnp.float32) * std_vd}
    _L1_xattn_all = _L1_xattn_setup()
    _L1_xattn_in = {k: v for k, v in _L1_xattn_all.items() if k in ('Wq', 'Wk', 'Wv', 'Wd')}
    del _L1_xattn_all

    def _L1_ffn_setup():
        import jax, jax.numpy as jnp
        import numpy as np
        NF4 = jnp.array([-1.0, -0.6961928009986877, -0.5250730514526367, -0.39491748809814453, -0.28444138169288635, -0.18477343022823334, -0.09105003625154495, 0.0, 0.07958029955625534, 0.16093020141124725, 0.24611230194568634, 0.33791524171829224, 0.44070982933044434, 0.5626170039176941, 0.7229568362236023, 1.0], dtype=jnp.float32)
        BLOCK = 64
        B, S, D, H, R = (2, 256, 512, 1376, 16)

        def dequant_nf4(codes, absmax, shape):
            vals = NF4[codes] * jnp.repeat(absmax, BLOCK)
            return vals.reshape(shape)
        key = jax.random.key(seed)
        ks = jax.random.split(key, 11)
        n_w = H * D
        return {'x1': jax.random.normal(ks[0], (B, S, D), dtype=jnp.float32), 'w_up_codes': jax.random.randint(ks[1], (n_w,), 0, 16, dtype=jnp.int32), 'w_up_absmax': jax.random.uniform(ks[2], (n_w // BLOCK,), dtype=jnp.float32) * 0.05, 'b_up': jax.random.normal(ks[3], (H,), dtype=jnp.float32) * 0.02, 'w_up_lora_a': jax.random.normal(ks[4], (D, R), dtype=jnp.float32) * 0.02, 'w_up_lora_b': jax.random.normal(ks[5], (R, H), dtype=jnp.float32) * 0.02, 'w_down_codes': jax.random.randint(ks[6], (n_w,), 0, 16, dtype=jnp.int32), 'w_down_absmax': jax.random.uniform(ks[7], (n_w // BLOCK,), dtype=jnp.float32) * 0.05, 'b_down': jax.random.normal(ks[8], (D,), dtype=jnp.float32) * 0.02, 'w_down_lora_a': jax.random.normal(ks[9], (H, R), dtype=jnp.float32) * 0.02, 'w_down_lora_b': jax.random.normal(ks[10], (R, D), dtype=jnp.float32) * 0.02}
    _L1_ffn_all = _L1_ffn_setup()
    _L1_ffn_in = {k: v for k, v in _L1_ffn_all.items() if k in ('w_up_codes', 'w_up_absmax', 'b_up', 'w_up_lora_a', 'w_up_lora_b', 'w_down_codes', 'w_down_absmax', 'b_down', 'w_down_lora_a', 'w_down_lora_b')}
    del _L1_ffn_all

    def _L2_xattn_setup():
        import jax, jax.numpy as jnp
        import numpy as np
        B, Q, D = (8, 64, 512)
        CTX = 512
        H, KV, HD = (16, 4, 96)
        G = H // KV
        key = jax.random.key(seed)
        ks = jax.random.split(key, 6)
        s = 0.02
        return {'latents': jax.random.normal(ks[0], (B, Q, D), jnp.float32), 'context': jax.random.normal(ks[1], (B, CTX, D), jnp.float32), 'Wq': jax.random.normal(ks[2], (H * HD, D), jnp.float32) * s, 'Wk': jax.random.normal(ks[3], (KV * HD, D), jnp.float32) * s, 'Wv': jax.random.normal(ks[4], (KV * HD, D), jnp.float32) * s, 'Wo': jax.random.normal(ks[5], (D, H * HD), jnp.float32) * s}
    _L2_xattn_all = _L2_xattn_setup()
    _L2_xattn_in = {k: v for k, v in _L2_xattn_all.items() if k in ('Wq', 'Wk', 'Wv', 'Wo')}
    del _L2_xattn_all

    def _L2_ffn_setup():
        import jax, jax.numpy as jnp
        import numpy as np
        R = 16
        NUM_EXPERTS = 8
        TOP_K = 2
        LORA_ALPHA = 32
        SCALING = LORA_ALPHA / R
        key = jax.random.key(seed)
        ks = jax.random.split(key, 6)
        d_in, d_out = (512, 512)
        x = jax.random.normal(ks[0], (4, 256, d_in), dtype=jnp.float32)
        W_base = jax.random.normal(ks[1], (d_out, d_in), dtype=jnp.float32) * 0.02
        b_base = jax.random.normal(ks[2], (d_out,), dtype=jnp.float32) * 0.02
        W_router = jax.random.normal(ks[3], (NUM_EXPERTS, d_in), dtype=jnp.float32) * 0.01
        A = jax.random.normal(ks[4], (NUM_EXPERTS, R, d_in), dtype=jnp.float32) * 0.02
        B = jax.random.normal(ks[5], (NUM_EXPERTS, d_out, R), dtype=jnp.float32) * 0.02
        return {'x': x, 'W_base': W_base, 'b_base': b_base, 'W_router': W_router, 'A': A, 'B': B}
    _L2_ffn_all = _L2_ffn_setup()
    _L2_ffn_in = {k: v for k, v in _L2_ffn_all.items() if k in ('W_base', 'b_base', 'W_router', 'A', 'B')}
    del _L2_ffn_all

    def _L3_xattn_setup():
        import jax, jax.numpy as jnp
        import numpy as np
        B, Q, K, D = (1, 128, 6404, 512)
        H, KVH, HD = (32, 8, 128)
        GROUPS = H // KVH
        EPS = 1e-05

        def _rmsnorm(x, w):
            xf = x.astype(jnp.float32)
            var = jnp.mean(xf * xf, axis=-1, keepdims=True)
            return (xf * jax.lax.rsqrt(var + EPS)).astype(x.dtype) * w
        key = jax.random.key(seed)
        ks = jax.random.split(key, 8)
        s = 0.02
        return {'hidden_states': jax.random.normal(ks[0], (B, Q, D), jnp.float32), 'cross_attention_states': jax.random.normal(ks[1], (B, K, D), jnp.float32), 'attention_mask': jnp.zeros((B, 1, Q, K), jnp.float32), 'Wq': jax.random.normal(ks[2], (H * HD, D), jnp.float32) * s, 'Wk': jax.random.normal(ks[3], (KVH * HD, D), jnp.float32) * s, 'Wv': jax.random.normal(ks[4], (KVH * HD, D), jnp.float32) * s, 'Wo': jax.random.normal(ks[5], (D, H * HD), jnp.float32) * s, 'q_norm_w': jnp.ones((HD,), jnp.float32), 'k_norm_w': jnp.ones((HD,), jnp.float32)}
    _L3_xattn_all = _L3_xattn_setup()
    _L3_xattn_in = {k: v for k, v in _L3_xattn_all.items() if k in ('Wq', 'Wk', 'Wv', 'Wo', 'q_norm_w', 'k_norm_w')}
    del _L3_xattn_all

    def _L3_ffn_setup():
        import jax, jax.numpy as jnp
        import numpy as np
        SCALING = 1.0 / 16.0
        key = jax.random.key(seed)
        k1, k2, k3, k4, k5 = jax.random.split(key, 5)
        B_, S, D_in, D_out, R = (4, 512, 512, 512, 16)
        x = jax.random.normal(k1, (B_, S, D_in), dtype=jnp.float32)
        W_q = jax.random.normal(k2, (D_out, D_in), dtype=jnp.float32) * 0.02
        A = jax.random.normal(k3, (D_out, R), dtype=jnp.float32) * 0.02
        B = jax.random.normal(k4, (R, D_in), dtype=jnp.float32) * 0.02
        bias = jax.random.normal(k5, (D_out,), dtype=jnp.float32) * 0.02
        return {'x': x, 'W_q': W_q, 'A': A, 'B': B, 'bias': bias}
    _L3_ffn_all = _L3_ffn_setup()
    _L3_ffn_in = {k: v for k, v in _L3_ffn_all.items() if k in ('W_q', 'A', 'B', 'bias')}
    del _L3_ffn_all
    return {'x': x, 'ctx_4096': ctx_4096, 'mask_1x1xSxS2_ff0': mask_1x1xSxS2_ff0, 'g_xattn': g_xattn, 'g_ffn': g_ffn, 'L0_xattn_Wq': _L0_xattn_in['Wq'], 'L0_xattn_bq': _L0_xattn_in['bq'], 'L0_xattn_Wkv': _L0_xattn_in['Wkv'], 'L0_xattn_bkv': _L0_xattn_in['bkv'], 'L0_xattn_Wo': _L0_xattn_in['Wo'], 'L0_xattn_bo': _L0_xattn_in['bo'], 'L0_ffn_weight': _L0_ffn_in['weight'], 'L0_ffn_bias': _L0_ffn_in['bias'], 'L0_ffn_scale': _L0_ffn_in['scale'], 'L0_ffn_ln_gamma': _L0_ffn_in['ln_gamma'], 'L0_ffn_ln_beta': _L0_ffn_in['ln_beta'], 'L0_ffn_quant_scale': _L0_ffn_in['quant_scale'], 'L1_xattn_Wq': _L1_xattn_in['Wq'], 'L1_xattn_Wk': _L1_xattn_in['Wk'], 'L1_xattn_Wv': _L1_xattn_in['Wv'], 'L1_xattn_Wd': _L1_xattn_in['Wd'], 'L1_ffn_w_up_codes': _L1_ffn_in['w_up_codes'], 'L1_ffn_w_up_absmax': _L1_ffn_in['w_up_absmax'], 'L1_ffn_b_up': _L1_ffn_in['b_up'], 'L1_ffn_w_up_lora_a': _L1_ffn_in['w_up_lora_a'], 'L1_ffn_w_up_lora_b': _L1_ffn_in['w_up_lora_b'], 'L1_ffn_w_down_codes': _L1_ffn_in['w_down_codes'], 'L1_ffn_w_down_absmax': _L1_ffn_in['w_down_absmax'], 'L1_ffn_b_down': _L1_ffn_in['b_down'], 'L1_ffn_w_down_lora_a': _L1_ffn_in['w_down_lora_a'], 'L1_ffn_w_down_lora_b': _L1_ffn_in['w_down_lora_b'], 'L2_xattn_Wq': _L2_xattn_in['Wq'], 'L2_xattn_Wk': _L2_xattn_in['Wk'], 'L2_xattn_Wv': _L2_xattn_in['Wv'], 'L2_xattn_Wo': _L2_xattn_in['Wo'], 'L2_ffn_W_base': _L2_ffn_in['W_base'], 'L2_ffn_b_base': _L2_ffn_in['b_base'], 'L2_ffn_W_router': _L2_ffn_in['W_router'], 'L2_ffn_A': _L2_ffn_in['A'], 'L2_ffn_B': _L2_ffn_in['B'], 'L3_xattn_Wq': _L3_xattn_in['Wq'], 'L3_xattn_Wk': _L3_xattn_in['Wk'], 'L3_xattn_Wv': _L3_xattn_in['Wv'], 'L3_xattn_Wo': _L3_xattn_in['Wo'], 'L3_xattn_q_norm_w': _L3_xattn_in['q_norm_w'], 'L3_xattn_k_norm_w': _L3_xattn_in['k_norm_w'], 'L3_ffn_W_q': _L3_ffn_in['W_q'], 'L3_ffn_A': _L3_ffn_in['A'], 'L3_ffn_B': _L3_ffn_in['B'], 'L3_ffn_bias': _L3_ffn_in['bias']}

def reference(x, ctx_4096, mask_1x1xSxS2_ff0, g_xattn, g_ffn, L0_xattn_Wq, L0_xattn_bq, L0_xattn_Wkv, L0_xattn_bkv, L0_xattn_Wo, L0_xattn_bo, L0_ffn_weight, L0_ffn_bias, L0_ffn_scale, L0_ffn_ln_gamma, L0_ffn_ln_beta, L0_ffn_quant_scale, L1_xattn_Wq, L1_xattn_Wk, L1_xattn_Wv, L1_xattn_Wd, L1_ffn_w_up_codes, L1_ffn_w_up_absmax, L1_ffn_b_up, L1_ffn_w_up_lora_a, L1_ffn_w_up_lora_b, L1_ffn_w_down_codes, L1_ffn_w_down_absmax, L1_ffn_b_down, L1_ffn_w_down_lora_a, L1_ffn_w_down_lora_b, L2_xattn_Wq, L2_xattn_Wk, L2_xattn_Wv, L2_xattn_Wo, L2_ffn_W_base, L2_ffn_b_base, L2_ffn_W_router, L2_ffn_A, L2_ffn_B, L3_xattn_Wq, L3_xattn_Wk, L3_xattn_Wv, L3_xattn_Wo, L3_xattn_q_norm_w, L3_xattn_k_norm_w, L3_ffn_W_q, L3_ffn_A, L3_ffn_B, L3_ffn_bias):
    import jax
    import jax.numpy as jnp

    def _L0_xattn_ref(query, kv, Wq, bq, Wkv, bkv, Wo, bo):
        import jax, jax.numpy as jnp
        import numpy as np
        HID = 512
        NHEAD = 32
        NKV = 8
        HDIM = 128
        G = NHEAD // NKV
        B, L, _ = query.shape
        Lk = kv.shape[1]
        scale = jnp.asarray(1.0 / np.sqrt(HDIM), query.dtype)
        q = (query @ Wq + bq).reshape(B, L, NKV, G, HDIM)
        k_, v_ = jnp.split(kv @ Wkv + bkv, 2, axis=-1)
        k = k_.reshape(B, Lk, NKV, HDIM)
        v = v_.reshape(B, Lk, NKV, HDIM)
        scores = jnp.einsum('blkgd,bmkd->bkglm', q, k) * scale
        attn = jax.nn.softmax(scores, axis=-1)
        o = jnp.einsum('bkglm,bmkd->blkgd', attn, v).reshape(B, L, NHEAD * HDIM)
        return o @ Wo + bo

    def _L0_ffn_ref(x, weight, bias, scale, ln_gamma, ln_beta, quant_scale):
        import jax, jax.numpy as jnp
        import numpy as np
        B, S, DIN, DOUT = (8, 256, 512, 512)
        THRESH = 0.1
        LN_EPS = 1e-05
        tern_w = jnp.where(jnp.abs(weight) < THRESH, 0.0, jnp.sign(weight))
        y = jnp.einsum('bsd,od->bso', x, tern_w) + bias
        y = y * scale
        mu = jnp.mean(y, axis=-1, keepdims=True)
        var = jnp.mean(jnp.square(y - mu), axis=-1, keepdims=True)
        y = (y - mu) * jax.lax.rsqrt(var + LN_EPS) * ln_gamma + ln_beta
        y = jnp.tanh(y / quant_scale)
        y = jnp.round(y * 127.0) / 127.0
        return y

    def _L1_xattn_ref(q, k, v, Wq, Wk, Wv, Wd):
        import jax, jax.numpy as jnp
        import numpy as np
        EMB_DIM = 512
        NHEADS = 32
        KVHEADS = 8
        HEAD_DIM = 128
        ROPE_BASE = 10000.0

        def _rope(x):
            B, H, S, D = x.shape
            inv_freq = 1.0 / ROPE_BASE ** (jnp.arange(0, D, 2, dtype=jnp.float32) / D)
            ang = jnp.arange(S, dtype=jnp.float32)[:, None] * inv_freq[None, :]
            cos = jnp.concatenate([jnp.cos(ang), jnp.cos(ang)], axis=-1)
            sin = jnp.concatenate([jnp.sin(ang), jnp.sin(ang)], axis=-1)
            x1, x2 = (x[..., :D // 2], x[..., D // 2:])
            rot = jnp.concatenate([-x2, x1], axis=-1)
            return x * cos + rot * sin
        B, Sq, _ = q.shape
        Skv = k.shape[1]
        queries = (q @ Wq.T).reshape(B, Sq, NHEADS, HEAD_DIM).transpose(0, 2, 1, 3)
        keys = (k @ Wk.T).reshape(B, Skv, KVHEADS, HEAD_DIM).transpose(0, 2, 1, 3)
        values = (v @ Wv.T).reshape(B, Skv, KVHEADS, HEAD_DIM).transpose(0, 2, 1, 3)
        queries = _rope(queries)
        keys = _rope(keys)
        exp = NHEADS // KVHEADS
        keys = jnp.repeat(keys, exp, axis=1)
        values = jnp.repeat(values, exp, axis=1)
        scale = HEAD_DIM ** (-0.5)
        scores = jnp.einsum('bhqd,bhkd->bhqk', queries, keys) * scale
        causal = jnp.tril(jnp.ones((Sq, Skv), dtype=bool))
        scores = jnp.where(causal[None, None], scores, jnp.finfo(scores.dtype).min)
        attn = jax.nn.softmax(scores, axis=-1)
        ctx = jnp.einsum('bhqk,bhkd->bhqd', attn, values)
        ctx = ctx.transpose(0, 2, 1, 3).reshape(B, Sq, NHEADS * HEAD_DIM)
        return ctx @ Wd.T

    def _L1_ffn_ref(x1, w_up_codes, w_up_absmax, b_up, w_up_lora_a, w_up_lora_b, w_down_codes, w_down_absmax, b_down, w_down_lora_a, w_down_lora_b):
        import jax, jax.numpy as jnp
        import numpy as np
        NF4 = jnp.array([-1.0, -0.6961928009986877, -0.5250730514526367, -0.39491748809814453, -0.28444138169288635, -0.18477343022823334, -0.09105003625154495, 0.0, 0.07958029955625534, 0.16093020141124725, 0.24611230194568634, 0.33791524171829224, 0.44070982933044434, 0.5626170039176941, 0.7229568362236023, 1.0], dtype=jnp.float32)
        BLOCK = 64
        B, S, D, H, R = (2, 256, 512, 1376, 16)

        def dequant_nf4(codes, absmax, shape):
            vals = NF4[codes] * jnp.repeat(absmax, BLOCK)
            return vals.reshape(shape)
        w_up = dequant_nf4(w_up_codes, w_up_absmax, (H, D)).T
        y1 = x1 @ w_up + b_up + x1 @ w_up_lora_a @ w_up_lora_b
        x2 = jax.nn.relu(y1)
        w_down = dequant_nf4(w_down_codes, w_down_absmax, (D, H)).T
        y2 = x2 @ w_down + b_down + x2 @ w_down_lora_a @ w_down_lora_b
        return y2

    def _L2_xattn_ref(latents, context, Wq, Wk, Wv, Wo):
        import jax, jax.numpy as jnp
        import numpy as np
        B, Q, D = (8, 64, 512)
        CTX = 512
        H, KV, HD = (16, 4, 96)
        G = H // KV
        b, q_len, _ = latents.shape
        hidden = jnp.concatenate([context, latents], axis=1)
        s_len = hidden.shape[1]
        q = (latents @ Wq.T).reshape(b, q_len, H, HD)
        k = (hidden @ Wk.T).reshape(b, s_len, KV, HD)
        v = (hidden @ Wv.T).reshape(b, s_len, KV, HD)
        q = q.transpose(0, 2, 1, 3).reshape(b, KV, G, q_len, HD)
        k = k.transpose(0, 2, 1, 3)
        v = v.transpose(0, 2, 1, 3)
        scale = 1.0 / jnp.sqrt(jnp.asarray(HD, q.dtype))
        scores = jnp.einsum('bkgqd,bksd->bkgqs', q, k) * scale
        attn = jax.nn.softmax(scores.astype(jnp.float32), axis=-1).astype(q.dtype)
        out = jnp.einsum('bkgqs,bksd->bkgqd', attn, v)
        out = out.reshape(b, H, q_len, HD).transpose(0, 2, 1, 3).reshape(b, q_len, H * HD)
        return out @ Wo.T

    def _L2_ffn_ref(x, W_base, b_base, W_router, A, B):
        import jax, jax.numpy as jnp
        import numpy as np
        R = 16
        NUM_EXPERTS = 8
        TOP_K = 2
        LORA_ALPHA = 32
        SCALING = LORA_ALPHA / R
        orig_shape = x.shape
        d_in = x.shape[-1]
        x_flat = x.reshape(-1, d_in)
        logits = x_flat @ W_router.T
        probs = jax.nn.softmax(logits, axis=-1)
        topk_probs, topk_idx = jax.lax.top_k(probs, TOP_K)
        topk_probs = topk_probs / jnp.sum(topk_probs, axis=-1, keepdims=True)
        onehot = jax.nn.one_hot(topk_idx, NUM_EXPERTS, dtype=x.dtype)
        combine = jnp.einsum('nk,nke->ne', topk_probs, onehot)
        h = jnp.einsum('nd,erd->ner', x_flat, A)
        hw = h * combine[:, :, None]
        expert_out = jnp.einsum('ner,eor->no', hw, B) * SCALING
        base_out = x_flat @ W_base.T + b_base
        out = base_out + expert_out
        return out.reshape(*orig_shape[:-1], W_base.shape[0])

    def _L3_xattn_ref(hidden_states, cross_attention_states, attention_mask, Wq, Wk, Wv, Wo, q_norm_w, k_norm_w):
        import jax, jax.numpy as jnp
        import numpy as np
        B, Q, K, D = (1, 128, 6404, 512)
        H, KVH, HD = (32, 8, 128)
        GROUPS = H // KVH
        EPS = 1e-05

        def _rmsnorm(x, w):
            xf = x.astype(jnp.float32)
            var = jnp.mean(xf * xf, axis=-1, keepdims=True)
            return (xf * jax.lax.rsqrt(var + EPS)).astype(x.dtype) * w
        bsz, q_len, _ = hidden_states.shape
        kv_len = cross_attention_states.shape[1]
        q = (hidden_states @ Wq.T).reshape(bsz, q_len, H, HD).transpose(0, 2, 1, 3)
        k = (cross_attention_states @ Wk.T).reshape(bsz, kv_len, KVH, HD).transpose(0, 2, 1, 3)
        v = (cross_attention_states @ Wv.T).reshape(bsz, kv_len, KVH, HD).transpose(0, 2, 1, 3)
        q = _rmsnorm(q, q_norm_w)
        k = jnp.repeat(k, GROUPS, axis=1)
        v = jnp.repeat(v, GROUPS, axis=1)
        k = _rmsnorm(k, k_norm_w)
        scale = 1.0 / np.sqrt(HD)
        scores = jnp.einsum('bhqd,bhkd->bhqk', q, k) * scale
        scores = scores + attention_mask[:, :, :, :kv_len]
        probs = jax.nn.softmax(scores.astype(jnp.float32), axis=-1).astype(q.dtype)
        out = jnp.einsum('bhqk,bhkd->bhqd', probs, v)
        out = out.transpose(0, 2, 1, 3).reshape(bsz, q_len, H * HD)
        return out @ Wo.T

    def _L3_ffn_ref(x, W_q, A, B, bias):
        import jax, jax.numpy as jnp
        import numpy as np
        SCALING = 1.0 / 16.0
        eff_w = W_q + SCALING * (A @ B)
        return jnp.einsum('bsi,oi->bso', x, eff_w) + bias
    x = x + jnp.tanh(g_xattn[0]) * _L0_xattn_ref(_layernorm(x, axis=-1), ctx_4096, L0_xattn_Wq, L0_xattn_bq, L0_xattn_Wkv, L0_xattn_bkv, L0_xattn_Wo, L0_xattn_bo)
    x = x + jnp.tanh(g_ffn[0]) * _L0_ffn_ref(_layernorm(x, axis=-1), L0_ffn_weight, L0_ffn_bias, L0_ffn_scale, L0_ffn_ln_gamma, L0_ffn_ln_beta, L0_ffn_quant_scale)
    x = x + jnp.tanh(g_xattn[1]) * _L1_xattn_ref(_layernorm(x, axis=-1), ctx_4096, ctx_4096, L1_xattn_Wq, L1_xattn_Wk, L1_xattn_Wv, L1_xattn_Wd)
    x = x + jnp.tanh(g_ffn[1]) * _L1_ffn_ref(_layernorm(x, axis=-1), L1_ffn_w_up_codes, L1_ffn_w_up_absmax, L1_ffn_b_up, L1_ffn_w_up_lora_a, L1_ffn_w_up_lora_b, L1_ffn_w_down_codes, L1_ffn_w_down_absmax, L1_ffn_b_down, L1_ffn_w_down_lora_a, L1_ffn_w_down_lora_b)
    x = x + jnp.tanh(g_xattn[2]) * _L2_xattn_ref(_layernorm(x, axis=-1), ctx_4096, L2_xattn_Wq, L2_xattn_Wk, L2_xattn_Wv, L2_xattn_Wo)
    x = x + jnp.tanh(g_ffn[2]) * _L2_ffn_ref(_layernorm(x, axis=-1), L2_ffn_W_base, L2_ffn_b_base, L2_ffn_W_router, L2_ffn_A, L2_ffn_B)
    x = x + jnp.tanh(g_xattn[3]) * _L3_xattn_ref(_layernorm(x, axis=-1), ctx_4096, mask_1x1xSxS2_ff0, L3_xattn_Wq, L3_xattn_Wk, L3_xattn_Wv, L3_xattn_Wo, L3_xattn_q_norm_w, L3_xattn_k_norm_w)
    x = x + jnp.tanh(g_ffn[3]) * _L3_ffn_ref(_layernorm(x, axis=-1), L3_ffn_W_q, L3_ffn_A, L3_ffn_B, L3_ffn_bias)
    return x

_drawn_inputs = setup_inputs


def setup_inputs(seed=0):
    import zlib

    import numpy as np

    out = dict(_drawn_inputs(seed))
    spreads = {'L0_xattn_bq': (0.0, 0.8),
     'L0_xattn_bkv': (0.0, 0.1),
     'L0_xattn_bo': (0.0, 0.1),
     'L0_ffn_bias': (0.0, 0.1),
     'L0_ffn_scale': (1.0, 0.6),
     'L0_ffn_ln_gamma': (1.0, 0.6),
     'L0_ffn_ln_beta': (0.0, 0.8),
     'L3_xattn_q_norm_w': (1.0, 0.6),
     'L3_xattn_k_norm_w': (1.0, 0.6)}
    factors = {'g_ffn': 24.936,
     'L0_xattn_Wq': 3.897,
     'L1_ffn_b_up': 8.0,
     'L1_ffn_w_up_lora_a': 5.045,
     'L1_ffn_w_up_lora_b': 5.132,
     'L1_ffn_b_down': 3.756,
     'L1_ffn_w_down_lora_a': 5.474,
     'L1_ffn_w_down_lora_b': 5.231,
     'L2_xattn_Wq': 7.389,
     'L2_xattn_Wk': 7.075,
     'L2_ffn_b_base': 4.268,
     'L3_ffn_A': 8.0,
     'L3_ffn_B': 8.0,
     'L3_ffn_bias': 4.034}
    for name, (base, spread) in spreads.items():
        noise = np.random.default_rng([zlib.crc32(name.encode()), seed]).standard_normal(out[name].shape)
        drawn = base * np.exp(spread * noise) if base else spread * noise
        out[name] = jnp.asarray(drawn.astype(out[name].dtype))
    for name, factor in factors.items():
        out[name] = (out[name] * factor).astype(out[name].dtype)
    return out
```

```python
from contextlib import ExitStack

import concourse.bass as bass
from concourse import mybir

F32 = mybir.dt.float32
F32R = mybir.dt.float32r
I32 = mybir.dt.int32
ALU = mybir.AluOpType
ACT = mybir.ActivationFunctionType
AX = mybir.AxisListType

P = 128
B = 2
SQ = 256
TOK = B * SQ
D = 512
DC = D // P
NT = TOK // P
CTX = 512
G4 = 4
EPS = 1e-5
NEG = -1e30
H1 = 1376
H1C = -(-H1 // P)
NE, RANK = 8, 16
NF4 = [-1.0, -0.6961928009986877, -0.5250730514526367, -0.39491748809814453, -0.28444138169288635,
       -0.18477343022823334, -0.09105003625154495, 0.0, 0.07958029955625534, 0.16093020141124725,
       0.24611230194568634, 0.33791524171829224, 0.44070982933044434, 0.5626170039176941,
       0.7229568362236023, 1.0]
DQ = 344
UP_PER_C = H1 // DQ
ROUND = 1.5 * 2.0 ** 23

ATTN = [
    dict(kind="bias", hd=128, groups=8, keys=512, nbuf=2, ahead=2,
         prep={(1, 1): ["k0"], (1, 2): ["k1"], (2, 0): ["v0"], (2, 1): ["v1"], (3, 0): ["t0"], (3, 1): ["t1"]}),
    dict(kind="rope", hd=128, groups=8, keys=256, nbuf=2, ahead=2,
         prep={(1, 1): ["k0"], (2, 1): ["v0"], (3, 1): ["t0"]}),
    dict(kind="plain", hd=96, groups=4, keys=768, nbuf=1, ahead=1,
         prep={(1, 0): ["k0"], (1, 1): ["k1"], (1, 2): ["k2"], (2, 0): ["v0"], (2, 1): ["v1"], (2, 2): ["t0"],
               (3, 0): ["v2"], (3, 1): ["t1"], (3, 2): ["t2"]}),
    dict(kind="rms", hd=128, groups=8, keys=512, nbuf=2, ahead=2,
         prep={(1, 1): ["k0"], (1, 2): ["k1", "m0"], (2, 0): ["m1", "b0"], (2, 1): ["b1"],
               (2, 2): ["v0"], (3, 0): ["v1", "t0"], (3, 1): ["t1"]}),
]


COUNTERS = ("wqA_dma wqB_dma wkv_dma wo_dma vec_dma wq_hi wq_lo wkv_hi wkv_lo wo_hi wo_lo "
            "q_mm q_hi q_lo q_f q_sum q_r s_mm s_nm s_mask s_max s_exp s_rec s_norm t_mm t_hi t_lo "
            "av_mm o_hi o_lo x_mm x_act x_free k_f k_hi k_lo k_r k_diag").split()


class Group:

    def __init__(self, off, loop=None, last=False, mul=2):
        self.off, self.loop, self.last, self.mul = off, loop, last, mul
        self.par = off % 2

    def at(self, per_group, const):
        if self.loop is None:
            return per_group * self.off + const
        assert per_group * self.off + const > 0
        return self.loop * (self.mul * per_group) + (per_group * self.off + const)

    def half(self, per_two, const):
        value = per_two * (self.off // 2) + const
        return value if self.loop is None else self.loop * (self.mul // 2 * per_two) + value

    def to(self, d, last=False):
        return Group(self.off + d, self.loop, last)


class Counter:

    def __init__(self, sem, base=0):
        self.sem, self.base = sem, base

    def wait(self, eng, value):
        if isinstance(value, int) and value <= 0:
            return
        eng.wait_ge(self.sem, value + self.base)

    def inc(self, ins, by=1):
        ins.then_inc(self.sem, by)


class Layer:

    def __init__(self, index, sems):
        cfg = ATTN[index]
        self.i, self.kind, self.hd, self.n = index, cfg["kind"], cfg["hd"], cfg["groups"]
        self.keys, self.nbuf, self.ahead, self.prep = cfg["keys"], cfg["nbuf"], cfg["ahead"], cfg["prep"]
        self.kt = self.keys // P
        self.scale = float(self.hd) ** -0.5
        self.rms, self.rope = self.kind == "rms", self.kind == "rope"
        self.masked = self.rms or self.rope
        self.flat = [u for slot in self.prep.values() for u in slot]
        every = [u for h in range(G4) for j in range(4) for u in self.plan(h, j)]
        prepared = set(self.flat)
        self.order = {u: i for i, u in enumerate(every)}
        self.last_order = {u: i for i, u in enumerate(
            [u for u in every if u not in prepared and u != ("q", G4 - 1)])}
        self.first_order = {u: i for i, u in enumerate([u for u in every if u[0] != "out"])}
        self.first = self.flat + ([("q", -1)] if self.rms else [])
        self.n_vec = dict(bias=16, rope=16, plain=0, rms=32)[self.kind]
        self.n_k = len([u for u in self.flat if u[0] == "k"])
        n = self.n
        self.total_x = len(self.first) - 4 + len(self.order) * (n - 1) + len(self.last_order) + 4
        act_uses = len([u for u in self.flat if u[0] in ("t" if self.masked else "kt")])
        total = dict(wqA_dma=32 * n, wqB_dma=32 * n, wkv_dma=16 * n, wo_dma=16 * n, vec_dma=self.n_vec,
                     wq_hi=4 * n, wq_lo=4 * n, wkv_hi=2 * n, wkv_lo=2 * n, wo_hi=4 * n, wo_lo=4 * n,
                     q_mm=4 * n, q_hi=4 * n, q_lo=4 * n, s_mm=16 * n, s_nm=0 if self.masked else 16 * n,
                     s_max=16 * n, s_exp=16 * n, s_rec=16 * n, s_norm=16 * n, t_mm=16 * n, t_hi=16 * n,
                     t_lo=16 * n, av_mm=8 * n, o_hi=4 * n, o_lo=4 * n, x_mm=self.total_x,
                     x_free=self.total_x, x_act=act_uses * n, s_mask=16 * n if self.masked else 0,
                     k_f=self.n_k * n if self.masked else 0, k_hi=self.n_k * n if self.masked else 0,
                     k_lo=self.n_k * n if self.masked else 0, q_f=4 * n if self.masked else 0,
                     q_sum=4 * n if self.rope else 0, q_r=4 * n if self.rms else 0,
                     k_r=2 * n if self.rms else 0, k_diag=2 * n if self.rms else 0)
        counters = [Counter(sems[name][0], sems[name][1]) for name in COUNTERS]
        (wqA_dma, wqB_dma, self.wkv_dma, self.wo_dma, self.vec_dma, self.wq_hi, self.wq_lo, self.wkv_hi,
         self.wkv_lo, self.wo_hi, self.wo_lo, self.q_mm, self.q_hi, self.q_lo, self.q_f, self.q_sum,
         self.q_r, self.s_mm, self.s_nm, self.s_mask, self.s_max, self.s_exp, self.s_rec, self.s_norm,
         self.t_mm, self.t_hi, self.t_lo, self.av_mm, self.o_hi, self.o_lo, self.x_mm, self.x_act,
         self.x_free, self.k_f, self.k_hi, self.k_lo, self.k_r, self.k_diag) = counters
        self.wq_dma = (wqA_dma, wqB_dma)
        for name in COUNTERS:
            sems[name] = (sems[name][0], sems[name][1] + total[name])

    def use(self, g, what):
        if g is None:
            k = self.first.index(what)
            return k, k % 2
        if what[0] == "end":
            k = self.total_x - 4 + what[1]
            return k, k % 2
        if g.loop is None and g.off == 0:
            k = len(self.first) + self.first_order[what]
            return k, k % 2
        order = self.last_order if g.last else self.order
        c = len(self.first) - 4 + order[what]
        return g.at(len(self.order), c), (c + len(self.order) * g.par) % 2

    def plan(self, h, j):
        out = [("out", j)] if h == 0 else []
        if self.rms and j == 1:
            out.append(("q", h))
        return out + self.prep.get((h, j), [])

    def slot_uses(self, g, h, j):
        order = self.last_order if g.last else self.order
        first = g.loop is None and g.off == 0
        return [u for u in self.plan(h, j) if u in order and not (first and u[0] == "out")]

    def open(self, j):
        return P if self.rope and j % 2 == 0 else self.keys

    def count(self, g, letters, what):
        mine = [u for u in self.flat if u[0] in letters]
        at = mine.index(what) + 1
        return at if g is None else g.at(len(mine), len(mine) + at)

    def step(self, g, h, j, d):
        k = 4 * h + j + d
        if k >= 16:
            return None if g.last else (g.to(1), (k - 16) // 4, k % 4)
        return g, k // 4, k % 4


def walk(eng, L, prologue, head, tail):
    prologue()
    head(Group(0), 0)
    pairs = (L.n - 2) // 2
    with eng.Fori(0, pairs) as i:
        for d in (0, 1):
            g = Group(d, i)
            for h in (1, 2, 3):
                head(g, h)
            head(g.to(1), 0)
    g = Group(L.n - 2)
    for h in (1, 2, 3):
        head(g, h)
    g = Group(L.n - 1, last=True)
    for h in range(G4):
        head(g, h)
    tail(g)


def program(nc, a, out, scratch_up, scratch_down):
    ctx = ExitStack()
    with ctx:
        def sb(name, shape, dt=F32):
            return ctx.enter_context(nc.sbuf_tensor(name, shape, dt))

        def pb(name, shape):
            return ctx.enter_context(nc.psum_tensor(name, shape, F32))

        def sem(name):
            return ctx.enter_context(nc.semaphore(name))

        x_sb = sb("x_sb", [P, NT, D])
        xnT_hi, xnT_lo = (sb(f"xnT_{z}", [P, DC, TOK], F32R) for z in ("hi", "lo"))
        cT_hi, cT_lo = (sb(f"cT_{z}", [P, DC, B * CTX], F32R) for z in ("hi", "lo"))
        ident = sb("ident", [P, P])
        ones = sb("ones", [P, P])
        gates = sb("gates", [P, 8])
        half = sb("half", [P, 4])
        ln_stat = sb("ln_stat", [P, NT, 6])
        ln_mv = sb("ln_mv", [P, NT, 2])
        ln_var = sb("ln_var", [P, NT])
        ln_rstd = sb("ln_rstd", [P, NT])
        xn_f = sb("xn_f", [P, 2, D])
        rows = sb("rows", [P, D])
        kT_hi, kT_lo = (sb(f"kT_{z}", [P, 2, 3 * CTX], F32R) for z in ("hi", "lo"))
        v_hi, v_lo = (sb(f"v_{z}", [P, 2, 12 * 96], F32R) for z in ("hi", "lo"))
        wq_f = sb("wq_f", [P, 2, DC * P])
        wq_hi, wq_lo = (sb(f"wq_{z}", [P, 2, DC * P], F32R) for z in ("hi", "lo"))
        wkv_f = sb("wkv_f", [P, 2, DC * P])
        wkv_hi, wkv_lo = (sb(f"wkv_{z}", [P, 2, DC * P], F32R) for z in ("hi", "lo"))
        wo_f = sb("wo_f", [P, G4, D])
        wo_hi, wo_lo = (sb(f"wo_{z}", [P, G4, D], F32R) for z in ("hi", "lo"))
        oT_hi, oT_lo = (sb(f"oT_{z}", [P, G4, TOK], F32R) for z in ("hi", "lo"))
        q_hi, q_lo = (sb(f"q_{z}", [P, 2, TOK], F32R) for z in ("hi", "lo"))
        p_sb = sb("p_sb", [P, 2048])
        pT_hi, pT_lo = (sb(f"pT_{z}", [P, 2, 6 * SQ], F32R) for z in ("hi", "lo"))
        scr = sb("scr", [P, 2, 512])
        qscr = sb("qscr", [P, 2, TOK])
        ksq = xn_f
        mask_sb = sb("mask_sb", [P, 2 * CTX])
        trig = mask_sb[:, 2 * SQ:4 * SQ].rearrange("p (z m) -> p z m", z=2)
        vecs = sb("vecs", [P, 64])
        nmax, nbias, rsum, rrec = (sb(z, [P, 4]) for z in ("nmax", "nbias", "rsum", "rrec"))
        q_ms, q_r, k_ms, k_r = (sb(z, [P, 2, 4]) for z in ("q_ms", "q_r", "k_ms", "k_r"))
        diag = rows[:, :].rearrange("p (a b) -> p a b", b=P)
        moe = xn_f[:, 0, 256:512].rearrange("p (i n) -> p i n", n=NT * NE)

        psS = pb("psS", [P, 2, 512])
        psT = pb("psT", [P, 2, 512])
        psO = pb("psO", [P, 512])
        psQ = pb("psQ", [P, 512])
        psX = pb("psX", [P, 2, 512])

        const_dma, gate_dma, gate_done, half_done = (sem(z) for z in
                                                     ("const_dma", "gate_dma", "gate_done", "half_done"))
        ctx_dma, ctx_lo = [sem("ctxA_dma"), sem("ctxB_dma")], sem("ctx_lo")
        ctx_hi = sem("ctx_hi")
        wait_met = sem("wait_met")
        dve_self = sem("dve_self")
        x_ready = sem("x_ready")
        ln_stats, ln_pow, ln_xn, ln_tp, ln_hi, ln_lo = (sem(z) for z in
                                                        ("ln_stats", "ln_pow", "ln_xn", "ln_tp", "ln_hi", "ln_lo"))
        row_dma, out_dma = sem("row_dma"), sem("out_dma")
        dq_dma, dq_out = [sem("dqA_dma"), sem("dqB_dma")], [sem("dqA_out"), sem("dqB_out")]
        dq_bits, dq_leafA, dq_leafB, dq_selA, dq_selB, dq_mm, dq_done = (
            sem(f"dq_{z}") for z in ("bits", "leafA", "leafB", "selA", "selB", "mm", "done"))
        f0_dma, f0_w, f0_mm, f0_var, f0_pow, f0_y, f0_tanh = (
            sem(f"f0_{z}") for z in ("dma", "w", "mm", "var", "pow", "y", "tanh"))
        f1_vec, f1_hi, f1_lo, f1_up, f1_relu, f1_yhi, f1_ylo, f1_down = (
            sem(f"f1_{z}") for z in ("vec", "hi", "lo", "up", "relu", "yhi", "ylo", "down"))
        f1_dma = [sem("f1A_dma"), sem("f1B_dma")]
        f2_dma, f2_ar, f2_h, f2_lg, f2_exp, f2_hw, f2_tp, f2_hwhi, f2_hwlo, f2_out = (
            sem(f"f2_{z}") for z in ("dma", "ar", "h", "lg", "exp", "hw", "tp", "hwhi", "hwlo", "out"))
        f3_dma, f3_ab, f3_w, f3_out = (sem(f"f3_{z}") for z in ("dma", "ab", "w", "out"))
        sems = {name: (sem(name), 0) for name in COUNTERS}
        layers = [Layer(i, sems) for i in range(4)]
        own = [0]

        def after(dve, ins):
            own[0] += 1
            ins.then_inc(dve_self, 1)
            dve.wait_ge(dve_self, own[0])

        def three(pe, dst, pairs, first=True, last=True):
            n, k = 3 * len(pairs), 0
            for (wh, wl), (mh, ml) in pairs:
                for w, m in ((wh, mh), (wl, mh), (wh, ml)):
                    mm = pe.matmul(dst, w, m, start=(first and k == 0), stop=(last and k == n - 1))
                    k += 1
            return mm

        def start_sync(sp):
            sp.dma_start(ident[:, :], a["c_ident"]).then_inc(const_dma, 16)
            sp.dma_start(ones[:, :], a["c_ones"]).then_inc(const_dma, 16)
            sp.dma_start(x_sb[:, :, :], a["x"].rearrange("b (t p) d -> p (b t) d", p=P)).then_inc(const_dma, 16)
            sp.dma_start(gates[:, 0:4], a["g_xattn"].partition_broadcast(P)).then_inc(gate_dma, 16)
            sp.dma_start(gates[:, 4:8], a["g_ffn"].partition_broadcast(P)).then_inc(gate_dma, 16)
            for c in range(DC):
                if c >= 2:
                    sp.wait_ge(ctx_lo, c - 1)
                sp.dma_start(p_sb[:, (c % 2) * 1024:(c % 2 + 1) * 1024],
                             a["ctxT"][:, c, :]).then_inc(ctx_dma[c % 2], 16)

        def start_vector(dve):
            dve.memset(half[:, :], -0.5).then_inc(half_done, 1)
            for c in range(DC):
                dve.wait_ge(ctx_dma[c % 2], 16 * (c // 2 + 1))
                f = p_sb[:, (c % 2) * 1024:(c % 2 + 1) * 1024]
                dve.tensor_copy(cT_hi[:, c, :], f).then_inc(ctx_hi, 1)
                dve.wait_ge(ctx_hi, c + 1)
                dve.tensor_tensor(cT_lo[:, c, :], f, cT_hi[:, c, :].bitcast(F32), ALU.subtract).then_inc(ctx_lo, 1)
            dve.wait_ge(ctx_lo, DC)

        def start_scalar(act):
            act.wait_ge(gate_dma, 32)
            act.activation(gates[:, :], gates[:, :], ACT.Tanh).then_inc(gate_done, 1)

        dq_codes, dq_bit = wq_f[:, :, :].bitcast(I32), p_sb[:, :].rearrange("p (i n) -> p i n", i=4).bitcast(I32)
        dq_amax, dq_low, dq_w = qscr, scr, xn_f
        dq_l, dq_r = rows, mask_sb
        DOWN0 = DC * UP_PER_C

        def dq_pieces(eng, do):
            with eng.Fori(0, DC) as c:
                for m in range(UP_PER_C):
                    do(Group(m, c, mul=UP_PER_C), c, m, True, P, DQ)
            with eng.Fori(0, (H1C - 1) // 2) as i:
                for m in range(2):
                    do(Group(DOWN0 + m, i, mul=2), i * 2 + m, m, False, P, D)
            do(Group(DOWN0 + H1C - 1), H1C - 1, 0, False, H1 - (H1C - 1) * P, D)

        def dq_source(name, c, m, up, rows_, cols):
            if up:
                return a[name + "_up"][bass.ds(c, 1), :, m * DQ:(m + 1) * DQ].rearrange("c p n -> (c p) n")
            return a[name + "_down"][bass.ds(c * P, rows_), :]

        def dq_sync(sp):
            def do(k, c, m, up, rows_, cols):
                par = k.off % 2
                sp.wait_ge(dq_done, k.at(1, 1))
                sp.dma_start(dq_codes[0:rows_, par, 0:cols], dq_source("codes", c, m, up, rows_, cols)).then_inc(dq_dma[par], 16)
                sp.dma_start(dq_amax[0:rows_, par, 0:cols], dq_source("amax", c, m, up, rows_, cols)).then_inc(dq_dma[par], 16)
                left = (a["lora_l_up"] if up else a["lora_l_down"])[:, bass.ds(c * P, rows_)]
                right = a["lora_r_up"][:, m * DQ:(m + 1) * DQ] if up else a["lora_r_down"]
                sp.dma_start(dq_l[0:RANK, par * P:par * P + rows_], left).then_inc(dq_dma[par], 16)
                sp.dma_start(dq_r[0:RANK, par * 512:par * 512 + cols], right).then_inc(dq_dma[par], 16)
            dq_pieces(sp, do)

        def dq_tensor(pe):
            def do(k, c, m, up, rows_, cols):
                par = k.off % 2
                pe.wait_ge(dq_dma[par], k.half(64, 64))
                pe.wait_ge(dq_done, k.at(1, 2))
                pe.matmul(psO[0:rows_, 0:cols], dq_l[0:RANK, par * P:par * P + rows_],
                          dq_r[0:RANK, par * 512:par * 512 + cols], start=True, stop=True).then_inc(dq_mm, 1)
            dq_pieces(pe, do)

        def dq_scalar(act):
            def do(k, c, m, up, rows_, cols):
                par = k.off % 2
                act.wait_ge(dq_bits, k.at(1, 1))
                for side, free, ready in ((0, dq_selA, dq_leafA), (8, dq_selB, dq_leafB)):
                    act.wait_ge(free, k.at(1, 1))
                    for q in range(4):
                        lo, hi = NF4[side + 2 * q], NF4[side + 2 * q + 1]
                        ins = act.activation(dq_leaf(side, q, par)[0:rows_, 0:cols], dq_bit[0:rows_, 0, 0:cols],
                                             ACT.Copy, scale=hi - lo, bias=lo)
                    ins.then_inc(ready, 1)
            dq_pieces(act, do)

        def dq_leaf(side, q, par):
            if side == 0:
                return [dq_low[:, par, :], psS[:, 0, :], psS[:, 1, :], psT[:, 0, :]][q]
            return [psT[:, 1, :], psX[:, 0, :], psX[:, 1, :], psQ[:, :]][q]

        def dq_vector(dve):
            dve.sem_inc(dq_done, 2)
            dve.sem_inc(dq_selA, 1)
            dve.sem_inc(dq_selB, 1)

            def do(k, c, m, up, rows_, cols):
                par = k.off % 2
                bit = [dq_bit[0:rows_, i, 0:cols] for i in range(4)]

                def leaf(side, q):
                    return dq_leaf(side, q, par)[0:rows_, 0:cols]

                dve.wait_ge(dq_dma[par], k.half(64, 64))
                for i in range(4):
                    ins = dve.tensor_scalar(bit[i], dq_codes[0:rows_, par, 0:cols], 1 << i, None, ALU.bitwise_and)
                ins.then_inc(dq_bits, 1)
                dve.wait_ge(dq_bits, k.at(1, 1))
                for side, ready, done in ((0, dq_leafA, dq_selA), (8, dq_leafB, dq_selB)):
                    dve.wait_ge(ready, k.at(1, 1))
                    dve.sem_inc(wait_met, 1)
                    dve.copy_predicated(leaf(side, 0), bit[1], leaf(side, 1))
                    dve.copy_predicated(leaf(side, 2), bit[1], leaf(side, 3)).then_inc(dq_s1, 1)
                    dve.wait_ge(dq_s1, k.at(2, 1 + side // 8))
                    dve.sem_inc(wait_met, 1)
                    ins = dve.copy_predicated(leaf(side, 0), bit[2], leaf(side, 2))
                    if side == 0:
                        ins.then_inc(done, 1)
                ins.then_inc(dq_s2, 1)
                dve.wait_ge(dq_s2, k.at(1, 1))
                dve.sem_inc(wait_met, 1)
                low = leaf(0, 0)
                dve.copy_predicated(low, bit[3], leaf(8, 0)).then_inc(dq_selB, 1)
                dve.wait_ge(dq_selB, k.at(1, 2))
                dve.tensor_tensor(low, low, dq_amax[0:rows_, par, 0:cols], ALU.mult).then_inc(dq_val, 1)
                dve.wait_ge(dq_val, k.at(1, 1))
                dve.wait_ge(dq_mm, k.at(1, 1))
                dve.wait_ge(dq_wfree, k.at(1, 1))
                dve.tensor_tensor(dq_w[0:rows_, par, 0:cols], low, psO[0:rows_, 0:cols], ALU.add).then_inc(dq_done, 1)
            dq_pieces(dve, do)

        def dq_gpsimd(pool):
            pool.sem_inc(dq_wfree, 2)

            def do(k, c, m, up, rows_, cols):
                par = k.off % 2
                pool.wait_ge(dq_done, k.at(1, 3))
                if up:
                    dst = scratch_up[bass.ds(c, 1), :, m * DQ:(m + 1) * DQ].rearrange("c p n -> (c p) n")
                else:
                    dst = scratch_down[bass.ds(c * P, rows_), :]
                pool.dma_start(dst, dq_w[0:rows_, par, 0:cols]).then_inc(dq_out[par], 16)
                pool.wait_ge(dq_out[par], k.half(16, 16))
                pool.sem_inc(dq_wfree, 1)
            dq_pieces(pool, do)

        dq_s1, dq_s2, dq_val, dq_wfree = (sem(f"dq_{z}") for z in ("s1", "s2", "val", "wfree"))
        DQ_PIECES = DOWN0 + H1C

        def ln_vector(dve, k):
            dve.wait_ge(x_ready, k + 1)
            if k == 0:
                dve.wait_ge(const_dma, 48)
            for t in range(NT):
                ins = dve.bn_stats(ln_stat[:, t, :], x_sb[:, t, :])
            after(dve, ins)
            for t in range(NT):
                ins = dve.bn_aggr(ln_mv[:, t, :], ln_stat[:, t, :])
            after(dve, ins)
            dve.tensor_scalar(ln_var[:, :], ln_mv[:, :, 1], EPS, None, ALU.add).then_inc(ln_stats, 1)
            dve.wait_ge(ln_pow, k + 1)

            def low(t):
                dve.wait_ge(ln_hi, NT * k + t + 1)
                cols = slice(t * P, (t + 1) * P)
                dve.tensor_tensor(xnT_lo[:, :, cols], psT[:, t % 2, :].rearrange("p (c n) -> p c n", c=DC),
                                  xnT_hi[:, :, cols].bitcast(F32), ALU.subtract).then_inc(ln_lo, 1)

            for t in range(NT):
                if t >= 2 or k >= 1:
                    dve.wait_ge(ln_tp, NT * k + t - 1)
                dve.tensor_scalar(xn_f[:, t % 2, :], x_sb[:, t, :], ln_mv[:, t, 0:1], ln_rstd[:, t:t + 1],
                                  ALU.subtract, ALU.mult).then_inc(ln_xn, 1)
                if t >= 1:
                    low(t - 1)
            low(NT - 1)

        def ln_gpsimd(pool, k):
            if k == 0:
                pool.wait_ge(half_done, 1)
            pool.wait_ge(ln_stats, k + 1)
            pool.tensor_tensor(ln_rstd[:, :], ln_var[:, :], half[:, :], ALU.pow).then_inc(ln_pow, 1)

        def ln_tensor(pe, k):
            if k == 0:
                pe.wait_ge(const_dma, 48)
            for t in range(NT):
                pe.wait_ge(ln_xn, NT * k + t + 1)
                if t >= 2 or k >= 1:
                    pe.wait_ge(ln_lo, NT * k + t - 1)
                for c in range(DC):
                    mm = pe.transpose(psT[:, t % 2, c * P:(c + 1) * P], xn_f[:, t % 2, c * P:(c + 1) * P],
                                      ident[:, :])
                mm.then_inc(ln_tp, 1)

        def ln_scalar(act, k):
            for t in range(NT):
                act.wait_ge(ln_tp, NT * k + t + 1)
                act.activation(xnT_hi[:, :, t * P:(t + 1) * P],
                               psT[:, t % 2, :].rearrange("p (c n) -> p c n", c=DC),
                               ACT.Copy).then_inc(ln_hi, 1)

        def flat(t):
            return t.rearrange("p a b -> p (a b)")

        def s_view(L, j):
            return flat(psS[:, :, :])[:, 0:L.keys] if L.nbuf == 1 else psS[:, j % 2, 0:L.keys]

        def t_view(L, j):
            v = flat(psT[:, :, :])[:, 0:L.keys] if L.nbuf == 1 else psT[:, j % 2, 0:L.open(j)]
            return v.rearrange("p (m q) -> p m q", q=P)

        def p_view(L, j):
            at = (j % 2) * 768 if L.nbuf == 1 else j * 512
            return p_sb[:, at:at + L.open(j)]

        def pT_view(L, z, j):
            b, t = j // 2, j % 2
            v = z[:, b, 0:L.kt * SQ].rearrange("p (m q) -> p m q", q=SQ)
            return v[:, 0:L.open(j) // P, t * P:(t + 1) * P]

        def w_jobs(L, g, h, j):
            out = []
            if j == 1 and not (g.last and h >= 2):
                out.append(("wq", (g.to(1) if h >= 2 else g), (h + 2) % 4))
            if h == 0 and j in (0, 2) and not g.last:
                out.append(("wkv", g.to(1), j // 2))
            if h in (1, 2) and j in (0, 2):
                out.append(("wo", g, 2 * (h - 1) + j // 2))
            return out

        def w_parts(L, kind, piece):
            n = DC * L.hd
            if kind == "wq":
                return [z[:, piece % 2, 0:n] for z in (wq_f, wq_hi, wq_lo)]
            if kind == "wkv":
                return [z[:, piece, 0:n] for z in (wkv_f, wkv_hi, wkv_lo)]
            return [z[0:L.hd, piece, :] for z in (wo_f, wo_hi, wo_lo)]

        def attn_sync(sp, L):
            names = a[f"attn{L.i}"]

            def load_wq(g, h):
                k = g.at(4, h)
                L.wq_lo.wait(sp, g.at(4, h - 1))
                n = DC * L.hd
                L.wq_dma[h % 2].inc(
                    sp.dma_start(wq_f[:, h % 2, 0:n], names["wq"][k, :, :]), 16)

            def load_wkv(g):
                L.wkv_lo.wait(sp, g.at(2, 0))
                L.wkv_dma.inc(sp.dma_start(wkv_f[:, :, 0:DC * L.hd], names["wkv"][g.at(1, 0), :, :, :]), 16)

            def load_wo(g):
                L.wo_lo.wait(sp, g.at(4, 0))
                L.wo_dma.inc(sp.dma_start(wo_f[0:L.hd, :, :], names["wo"][g.at(1, 0), :, :, :]), 16)

            sp.wait_ge(x_ready, 2 * L.i + 1)
            load_wkv(Group(0))
            load_wq(Group(0), 0)
            load_wq(Group(0), 1)
            if "vecs" in names:
                L.vec_dma.inc(sp.dma_start(vecs[:, 0:names["vecs"].shape[1]], names["vecs"]), 16)
            if L.masked:
                L.vec_dma.inc(sp.dma_start(mask_sb[:, 0:names["mask"].shape[1]], names["mask"]), 16)
            if L.i == 0:
                sp.dma_start(rows[:, :], a["L0_xattn_bo"].partition_broadcast(P)).then_inc(row_dma, 16)

            def head(g, h):
                if not (g.last and h >= 2):
                    load_wq(g.to(1) if h >= 2 else g, (h + 2) % 4)
                if h == 0 and not g.last:
                    load_wkv(g.to(1))
                if h == 0:
                    load_wo(g)

            walk(sp, L, lambda: None, head, lambda g: None)

        def attn_tensor(pe, L):
            hd = L.hd

            def q_proj(g, h):
                L.wq_lo.wait(pe, g.at(4, h + 1))
                (L.q_f if L.rope else L.q_lo).wait(pe, g.at(4, h) if g.off or g.loop is not None or h else 0)
                L.q_mm.inc(three(pe, psQ[0:hd, :], [
                    ([z[:, h % 2, c * hd:(c + 1) * hd] for z in (wq_hi, wq_lo)],
                     (xnT_hi[:, c, :], xnT_lo[:, c, :])) for c in range(DC)]))

            def scores(g, h, j):
                b, t = j // 2, j % 2
                if j == 0:
                    L.q_lo.wait(pe, g.at(4, h + 1))
                    if h == 0:
                        if L.masked:
                            L.k_lo.wait(pe, g.at(L.n_k, L.n_k))
                        else:
                            prev = g.to(-1) if g.off else None
                            L.x_free.wait(pe, L.use(prev, f"k{L.n_k - 1}")[0] + 1)
                free = L.s_mask if L.masked else L.s_exp
                free.wait(pe, g.at(16, 4 * h + j - L.nbuf + 1))
                q = [z[0:hd, h % 2, b * SQ + t * P:b * SQ + (t + 1) * P] for z in (q_hi, q_lo)]
                if L.kind == "plain":
                    parts = [(b * CTX, CTX, 0), (2 * CTX + b * SQ, SQ, CTX)]
                else:
                    parts = [(b * L.keys, L.keys, 0)]
                for col, n, to in parts:
                    mm = three(pe, s_view(L, j)[:, to:to + n],
                               [(q, [z[0:hd, g.par, col:col + n] for z in (kT_hi, kT_lo)])])
                L.s_mm.inc(mm)

            def transposes(g, h, j):
                L.s_norm.wait(pe, g.at(16, 4 * h + j + 1))
                L.t_lo.wait(pe, g.at(16, 4 * h + j - L.nbuf + 1) if (g.off or g.loop is not None or h or j >= L.nbuf)
                            else 0)
                for m in range(L.open(j) // P):
                    mm = pe.transpose(t_view(L, j)[:, m, :], p_view(L, j)[:, m * P:(m + 1) * P], ident[:, :])
                L.t_mm.inc(mm)

            def weighted_v(g, h, b):
                L.t_lo.wait(pe, g.at(16, 4 * h + 2 * b + 2))
                if b == 0:
                    L.o_lo.wait(pe, g.at(4, h) if g.off or g.loop is not None or h else 0)
                    if h == 0:
                        prev = g.to(-1) if g.off else None
                        L.x_free.wait(pe, L.use(prev, L.flat[-1])[0] + 1)
                pairs = []
                for m in range(L.kt):
                    if L.kind == "plain":
                        tile = 4 * b + m if m < 4 else 8 + 2 * b + (m - 4)
                    else:
                        tile = L.kt * b + m
                    pairs.append(([z[:, g.par, tile * hd:(tile + 1) * hd] for z in (v_hi, v_lo)],
                                  [z[:, b, m * SQ:(m + 1) * SQ] for z in (pT_hi, pT_lo)]))
                L.av_mm.inc(three(pe, psO[0:hd, b * SQ:(b + 1) * SQ], pairs))

            def use(g, what, gp):
                k, bank = L.use(g, what)
                if not (isinstance(k, int) and k < 2):
                    L.x_free.wait(pe, k - 1)
                X = psX[:, bank, :]
                kind, i = what[0], int(what[1])
                if kind in ("out", "end"):
                    L.o_lo.wait(pe, gp.at(4, 4))
                    L.wo_lo.wait(pe, gp.at(4, 4))
                    mm = three(pe, X, [([z[0:hd, h, i * P:(i + 1) * P] for z in (oT_hi, oT_lo)],
                                        [z[0:hd, h, :] for z in (wo_hi, wo_lo)]) for h in range(G4)])
                elif kind in "kv":
                    L.wkv_lo.wait(pe, gp.at(2, 1 if kind == "k" else 2))
                    pairs = []
                    for c in range(DC):
                        w = [z[:, int(kind == "v"), c * hd:(c + 1) * hd] for z in (wkv_hi, wkv_lo)]
                        if L.rope:
                            m = [z[:, c, :].rearrange("p (b m) -> p b m", b=B)[:, :, 0:L.keys] for z in (cT_hi, cT_lo)]
                        elif i == 2:
                            m = [z[:, c, :] for z in (xnT_hi, xnT_lo)]
                        else:
                            m = [z[:, c, i * CTX:(i + 1) * CTX] for z in (cT_hi, cT_lo)]
                        pairs.append((w, m))
                    dst = X[0:hd, :].rearrange("p (b m) -> p b m", b=B) if L.rope else X[0:hd, :]
                    mm = three(pe, dst, pairs)
                elif kind == "t":
                    L.x_free.wait(pe, L.use(g, f"v{i}")[0] + 1)
                    for m in range(4):
                        mm = pe.transpose(X[:, m * hd:(m + 1) * hd], scr[0:hd, i % 2, m * P:(m + 1) * P],
                                          ident[0:hd, 0:hd])
                elif kind == "m":
                    L.k_f.wait(pe, L.count(g, "k", f"k{i}"))
                    for m in range(4):
                        mm = pe.matmul(X[:, m:m + 1], ksq[:, i, m * P:(m + 1) * P], ones[:, 0:1],
                                       start=True, stop=True)
                elif kind == "b":
                    L.k_diag.wait(pe, L.count(g, "b", what))
                    mm = pe.matmul(X, ones[:, :], diag[:, :, :].rearrange("p a b -> p (a b)"), start=True, stop=True)
                else:
                    h = what[1] + 1
                    L.q_f.wait(pe, (Group(0) if g is None else g).at(4, h + 1))
                    for m in range(4):
                        mm = pe.matmul(X[:, m:m + 1], qscr[:, h % 2, m * P:(m + 1) * P], ones[:, 0:1],
                                       start=True, stop=True)
                L.x_mm.inc(mm)

            def prologue():
                q_proj(Group(0), 0)
                for u in L.first:
                    use(None, u, Group(0))
                q_proj(Group(0), 1)
                for j in range(L.ahead):
                    scores(Group(0), 0, j)

            def head(g, h):
                for j in range(4):
                    nxt = L.step(g, h, j, L.ahead)
                    if nxt:
                        scores(*nxt)
                    transposes(g, h, j)
                    if j == 2:
                        weighted_v(g, h, 0)
                    for u in L.slot_uses(g, h, j):
                        use(g, u, g.to(-1) if u[0] == "out" else g.to(1))
                    if j == 3:
                        if L.step(g, h, 0, 8):
                            q_proj(*L.step(g, h, 0, 8)[:2])
                        weighted_v(g, h, 1)

            def tail(g):
                for t in range(NT):
                    use(g, ("end", t), g)

            walk(pe, L, prologue, head, tail)

        def rotated(dve, src, dst):
            h = P // 2
            src = src.rearrange("p (b m) -> p b m", b=B)
            cos, sin = (trig[:, i, :].unsqueeze(1).broadcast_to([P, B, SQ]) for i in (0, 1))
            by_cos, by_sin = (dst[:, i, :].rearrange("p (b m) -> p b m", b=B) for i in (0, 1))
            dve.tensor_tensor(by_cos, src, cos, ALU.mult)
            dve.tensor_tensor(by_sin[0:h], src[h:P], sin[h:P], ALU.mult)
            return dve.tensor_tensor(by_sin[h:P], src[0:h], sin[0:h], ALU.mult)

        def attn_vector(dve, L):
            hd = L.hd
            gate = gates[:, L.i:L.i + 1]
            late = []

            def row_max(g, h, j):
                k = 4 * h + j
                L.s_mm.wait(dve, g.at(16, k + 1))
                if L.masked:
                    if L.rms and j == 0:
                        L.q_r.wait(dve, g.at(4, h + 1))
                    scale = q_r[:, h % 2, j:j + 1] if L.rms else L.scale
                    t = j % 2
                    L.s_mask.inc(dve.scalar_tensor_tensor(p_view(L, j), s_view(L, j)[:, 0:L.open(j)], scale,
                                                          mask_sb[:, t * L.keys:t * L.keys + L.open(j)],
                                                          ALU.mult, ALU.add))
                    L.s_mask.wait(dve, g.at(16, k + 1))
                    L.s_max.inc(dve.tensor_reduce(nbias[:, j:j + 1], p_view(L, j), AX.X, ALU.max, negate=True))
                else:
                    L.s_nm.inc(dve.tensor_reduce(nmax[:, j:j + 1], s_view(L, j), AX.X, ALU.max, negate=True))
                    L.s_nm.wait(dve, g.at(16, k + 1))
                    L.s_max.inc(dve.tensor_scalar(nbias[:, j:j + 1], nmax[:, j:j + 1], L.scale, None, ALU.mult))

            def row_recip(g, h, j):
                L.s_exp.wait(dve, g.at(16, 4 * h + j + 1))
                L.s_rec.inc(dve.reciprocal(rrec[:, j:j + 1], rsum[:, j:j + 1]))

            def pT_low(g, h, j):
                L.t_hi.wait(dve, g.at(16, 4 * h + j + 1))
                L.t_lo.inc(dve.tensor_tensor(pT_view(L, pT_lo, j), t_view(L, j), pT_view(L, pT_hi, j).bitcast(F32),
                                             ALU.subtract))

            def q_front(g, h):
                L.q_mm.wait(dve, g.at(4, h + 1))
                L.q_f.inc(rotated(dve, psQ[:, :], qscr))

            def q_low(g, h):
                L.q_hi.wait(dve, g.at(4, h + 1))
                lo, hi, src = q_lo[0:hd, h % 2, :], q_hi[0:hd, h % 2, :].bitcast(F32), psQ[0:hd, :]
                if L.kind == "bias":
                    col = g.at(4, h) if g.off or g.loop is not None or h else 0
                    ins = dve.scalar_tensor_tensor(lo, src, vecs[:, bass.ds(col, 1)], hi, ALU.add, ALU.subtract)
                elif L.rms:
                    ins = dve.scalar_tensor_tensor(lo, src, vecs[:, 0:1], hi, ALU.mult, ALU.subtract)
                else:
                    ins = dve.tensor_tensor(lo, qscr[:, 0, :] if L.rope else src, hi, ALU.subtract)
                L.q_lo.inc(ins)

            def o_low(g, h):
                L.o_hi.wait(dve, g.at(4, h + 1))
                L.o_lo.inc(dve.tensor_tensor(oT_lo[0:hd, h, :], psO[0:hd, :], oT_hi[0:hd, h, :].bitcast(F32),
                                             ALU.subtract))

            def k_low(g, i, kpar):
                L.k_hi.wait(dve, L.count(g, "k", f"k{i}"))
                cols = slice(i * 512, (i + 1) * 512)
                L.k_lo.inc(dve.tensor_tensor(kT_lo[:, kpar, cols], scr[:, i, :], kT_hi[:, kpar, cols].bitcast(F32),
                                             ALU.subtract))

            def use(g, what, gp):
                k, bank = L.use(g, what)
                X = psX[:, bank, :]
                kind, i = what[0], int(what[1])
                kpar = gp.par
                cols = slice(i * 512, (i + 1) * 512)
                act_letters = "t" if L.masked else "kt"
                if kind == "t" or (kind == "k" and not L.masked):
                    L.x_act.wait(dve, L.count(g, act_letters, what))
                elif kind == "k" and L.rms:
                    L.k_f.wait(dve, L.count(g, "k", what))
                else:
                    L.x_mm.wait(dve, k + 1)
                if kind == "v" and L.masked:
                    L.k_lo.wait(dve, L.count(g, "k", f"k{i}"))
                if kind in ("out", "end"):
                    ins = dve.scalar_tensor_tensor(x_sb[:, i, :], X, gate, x_sb[:, i, :], ALU.mult, ALU.add)
                elif kind == "k" and L.kind == "bias":
                    bk = vecs[:, bass.ds(gp.at(1, 4 * L.n), 1)]
                    ins = dve.scalar_tensor_tensor(kT_lo[:, kpar, cols], X, bk, kT_hi[:, kpar, cols].bitcast(F32),
                                                   ALU.add, ALU.subtract)
                elif kind == "k" and L.kind == "plain":
                    ins = dve.tensor_tensor(kT_lo[0:hd, kpar, cols], X[0:hd, :], kT_hi[0:hd, kpar, cols].bitcast(F32),
                                            ALU.subtract)
                elif kind == "k" and L.rope:
                    ins = rotated(dve, X, scr)
                    late.append((g, i, kpar))
                elif kind == "k":
                    ins = dve.tensor_scalar(scr[:, i, :], X, vecs[:, 1:2], None, ALU.mult)
                elif kind == "m":
                    ins = dve.tensor_scalar(k_ms[:, i, :], X[:, 0:4], 1.0 / hd, EPS, ALU.mult, ALU.add)
                elif kind == "b":
                    ins = dve.tensor_tensor(scr[:, i, :], scr[:, i, :], X, ALU.mult)
                    late.append((g, i, kpar))
                elif kind == "v" and L.kind == "bias":
                    bv = vecs[:, bass.ds(gp.at(1, 5 * L.n), 1)]
                    ins = dve.tensor_scalar(scr[:, i % 2, :], X, bv, None, ALU.add)
                elif kind == "v":
                    ins = dve.tensor_copy(scr[0:hd, i % 2, :], X[0:hd, :])
                elif kind == "t":
                    c = slice(i * 4 * hd, (i + 1) * 4 * hd)
                    ins = dve.tensor_tensor(v_lo[:, kpar, c], X[:, 0:4 * hd], v_hi[:, kpar, c].bitcast(F32),
                                            ALU.subtract)
                else:
                    ins = dve.tensor_scalar(q_ms[:, (what[1] + 1) % 2, :], X[:, 0:4], EPS * hd, None, ALU.add)
                L.x_free.inc(ins)

            def do_late(end=B):
                while late and late[0][1] < end:
                    k_low(*late.pop(0))

            def prologue():
                L.vec_dma.wait(dve, L.n_vec)
                if L.i == 0:
                    dve.wait_ge(row_dma, 16)
                    dve.wait_ge(gate_done, 1)
                    for t in range(NT):
                        ins = dve.scalar_tensor_tensor(x_sb[:, t, :], rows[:, :], gate, x_sb[:, t, :],
                                                       ALU.mult, ALU.add)
                    after(dve, ins)
                if L.rope:
                    for z in (pT_hi, pT_lo):
                        dve.memset(z[:, :, SQ:SQ + P].bitcast(F32), 0.0)
                    q_front(Group(0), 0)
                q_low(Group(0), 0)
                for u in L.first:
                    if u[0] == "v":
                        do_late()
                    use(None, u, Group(0))
                (q_front if L.rope else q_low)(Group(0), 1)
                for j in range(L.ahead):
                    row_max(Group(0), 0, j)
                for j in range(L.ahead):
                    row_recip(Group(0), 0, j)

            def head(g, h):
                for j in range(4):
                    nxt = L.step(g, h, j, L.ahead)
                    if nxt:
                        row_max(*nxt)
                    pT_low(g, h, j)
                    if nxt:
                        row_recip(*nxt)
                    if j == 0 and (h or g.off or g.loop is not None):
                        o_low(*((g, h - 1) if h else (g.to(-1), 3)))
                    if j == 1 and L.rope and L.step(g, h, 0, 4):
                        q_low(*L.step(g, h, 0, 4)[:2])
                    before = list(late)
                    for u in L.slot_uses(g, h, j):
                        if u[0] == "v":
                            do_late(int(u[1]) + 1)
                        use(g, u, g.to(-1) if u[0] == "out" else g.to(1))
                    while late and late[0] in before:
                        k_low(*late.pop(0))
                    if j == 3 and L.step(g, h, 0, 8):
                        (q_front if L.rope else q_low)(*L.step(g, h, 0, 8)[:2])

            def tail(g):
                o_low(g, 3)
                for t in range(NT):
                    use(g, ("end", t), g)
                L.x_free.wait(dve, L.total_x)
                dve.sem_inc(x_ready, 1)

            walk(dve, L, prologue, head, tail)

        def attn_scalar(act, L):
            hd = L.hd
            late = []

            def w_high(kind, g, piece):
                f, hi, lo = w_parts(L, kind, piece)
                if kind == "wq":
                    L.wq_dma[piece % 2].wait(act, g.at(32, 16 * (piece // 2 + 1)))
                    L.q_mm.wait(act, g.at(4, piece - 1) if g.off or g.loop is not None or piece > 1 else 0)
                    L.wq_hi.inc(act.activation(hi, f, ACT.Copy))
                elif kind == "wkv":
                    L.wkv_dma.wait(act, g.at(16, 16))
                    L.wkv_hi.inc(act.activation(hi, f, ACT.Copy))
                else:
                    L.wo_dma.wait(act, g.at(16, 16))
                    L.wo_hi.inc(act.activation(hi, f, ACT.Copy))

            def row_exp(g, h, j):
                L.s_max.wait(act, g.at(16, 4 * h + j + 1))
                src = p_view(L, j) if L.masked else s_view(L, j)
                L.s_exp.inc(act.activation(p_view(L, j), src, ACT.Exp, bias=nbias[:, j:j + 1],
                                           scale=1.0 if L.masked else L.scale, accum_out=rsum[:, j:j + 1]))

            def pT_high(g, h, j):
                L.t_mm.wait(act, g.at(16, 4 * h + j + 1))
                L.av_mm.wait(act, g.at(8, 2 * h + j // 2 - 1) if g.off or g.loop is not None or h else 0)
                L.t_hi.inc(act.activation(pT_view(L, pT_hi, j), t_view(L, j), ACT.Copy))

            def q_high(g, h):
                dst = q_hi[0:hd, h % 2, :]
                if L.rope:
                    L.q_sum.wait(act, g.at(4, h + 1))
                    ins = act.activation(dst, qscr[:, 0, :], ACT.Copy)
                else:
                    L.q_mm.wait(act, g.at(4, h + 1))
                    if L.rms:
                        L.q_f.inc(act.activation(qscr[:, h % 2, :], psQ[:, :], ACT.Square))
                        ins = act.activation(dst, psQ[:, :], ACT.Copy, scale=vecs[:, 0:1])
                    elif L.kind == "bias":
                        col = g.at(4, h) if g.off or g.loop is not None or h else 0
                        act.sem_inc(wait_met, 1)
                        ins = act.activation(dst, psQ[:, :], ACT.Identity, bias=vecs[:, bass.ds(col, 1)])
                    else:
                        ins = act.activation(dst, psQ[0:hd, :], ACT.Copy)
                L.q_hi.inc(ins)

            def o_high(g, h):
                L.av_mm.wait(act, g.at(8, 2 * h + 2))
                if h == 0 and (g.off or g.loop is not None):
                    L.x_mm.wait(act, L.use(g, ("out", 3))[0] + 1)
                L.o_hi.inc(act.activation(oT_hi[0:hd, h, :], psO[0:hd, :], ACT.Copy))

            def use(g, what, gp):
                k, bank = L.use(g, what)
                X = psX[:, bank, :]
                kind, i = what[0], int(what[1])
                cols = slice(i * 512, (i + 1) * 512)
                if kind == "k" and L.rms:
                    L.x_mm.wait(act, k + 1)
                    L.k_f.inc(act.activation(ksq[:, i, :], X, ACT.Square))
                elif (kind == "k" and L.rope) or kind == "b":
                    if L.rope:
                        L.k_f.wait(act, L.count(g, "k", what))
                    else:
                        L.x_free.wait(act, k + 1)
                    L.k_hi.inc(act.activation(kT_hi[:, gp.par, cols], scr[:, i, :], ACT.Copy))
                elif kind == "k":
                    L.x_mm.wait(act, k + 1)
                    dst = kT_hi[0:hd, gp.par, cols]
                    if L.kind == "bias":
                        act.sem_inc(wait_met, 1)
                        ins = act.activation(dst, X, ACT.Identity, bias=vecs[:, bass.ds(gp.at(1, 4 * L.n), 1)])
                    else:
                        ins = act.activation(dst, X[0:hd, :], ACT.Copy)
                    L.x_act.inc(ins)
                elif kind == "t":
                    L.x_mm.wait(act, k + 1)
                    L.x_act.inc(act.activation(v_hi[:, gp.par, i * 4 * hd:(i + 1) * 4 * hd], X[:, 0:4 * hd],
                                               ACT.Copy))

            def prologue():
                for kind, piece in (("wq", 0), ("wkv", 0), ("wkv", 1), ("wq", 1)):
                    w_high(kind, Group(0), piece)
                L.vec_dma.wait(act, L.n_vec)
                q_high(Group(0), 0)
                for u in L.first:
                    use(None, u, Group(0))
                if not L.rope:
                    q_high(Group(0), 1)
                for j in range(L.ahead):
                    row_exp(Group(0), 0, j)

            def head(g, h):
                for j in range(4):
                    pT_high(g, h, j)
                    nxt = L.step(g, h, j, L.ahead)
                    if nxt:
                        row_exp(*nxt)
                    if j == 1 and L.rope and L.step(g, h, 0, 4):
                        q_high(*L.step(g, h, 0, 4)[:2])
                    while late:
                        use(*late.pop(0))
                    for u in L.slot_uses(g, h, j):
                        if u[0] == "b" or (u[0] == "k" and L.rope):
                            late.append((g, u, g.to(1)))
                        elif u[0] not in ("out", "q"):
                            use(g, u, g.to(1))
                    for kind, wg, piece in w_jobs(L, g, h, j):
                        w_high(kind, wg, piece)
                    if j == 3:
                        if L.step(g, h, 0, 8) and not L.rope:
                            q_high(*L.step(g, h, 0, 8)[:2])
                        o_high(g, h)

            walk(act, L, prologue, head, lambda g: None)

        def attn_gpsimd(pool, L):
            def norm(g, h, j):
                L.s_rec.wait(pool, g.at(16, 4 * h + j + 1))
                L.s_norm.inc(pool.tensor_tensor(p_view(L, j), p_view(L, j),
                                                rrec[:, j:j + 1].broadcast_to([P, L.open(j)]), ALU.mult))

            def w_low(kind, g, piece):
                f, hi, lo = w_parts(L, kind, piece)
                if kind == "wq":
                    L.wq_hi.wait(pool, g.at(4, piece + 1))
                    L.wq_lo.inc(pool.tensor_tensor(lo, f, hi.bitcast(F32), ALU.subtract))
                elif kind == "wkv":
                    L.wkv_hi.wait(pool, g.at(2, piece + 1))
                    L.wkv_lo.inc(pool.tensor_tensor(lo, f, hi.bitcast(F32), ALU.subtract))
                else:
                    L.wo_hi.wait(pool, g.at(4, piece + 1))
                    L.wo_lo.inc(pool.tensor_tensor(lo, f, hi.bitcast(F32), ALU.subtract))

            def q_sum(g, h):
                L.q_f.wait(pool, g.at(4, h + 1))
                L.q_sum.inc(pool.tensor_tensor(qscr[:, 0, :], qscr[:, 0, :], qscr[:, 1, :], ALU.add))

            def use(g, what):
                if what[0] not in "kmq" or what[0] == "out":
                    return
                k, _ = L.use(g, what)
                if what[0] == "k" and L.rope:
                    L.x_free.wait(pool, k + 1)
                    L.k_f.inc(pool.tensor_tensor(scr[:, 0, :], scr[:, 0, :], scr[:, 1, :], ALU.add))
                elif what[0] == "m":
                    i = int(what[1])
                    L.x_free.wait(pool, k + 1)
                    L.k_r.inc(pool.tensor_tensor(k_r[:, i, :], k_ms[:, i, :], half[:, 0:4], ALU.pow))
                    L.k_r.wait(pool, L.count(g, "m", what))
                    if i:
                        L.x_mm.wait(pool, L.use(g, "b0")[0] + 1)
                    L.k_diag.inc(pool.tensor_tensor(diag[:, :, :], ident[:, :].unsqueeze(1).broadcast_to([P, 4, P]),
                                                    k_r[:, i, :].unsqueeze(2).broadcast_to([P, 4, P]), ALU.mult))
                elif what[0] == "q":
                    h = what[1] + 1
                    L.x_free.wait(pool, k + 1)
                    L.q_r.inc(pool.tensor_tensor(q_r[:, h % 2, :], q_ms[:, h % 2, :], half[:, 0:4], ALU.pow))

            def prologue():
                if L.i == 0:
                    pool.wait_ge(half_done, 1)
                for kind, piece in (("wq", 0), ("wkv", 0), ("wkv", 1), ("wq", 1)):
                    w_low(kind, Group(0), piece)
                if L.rope:
                    q_sum(Group(0), 0)
                for u in L.first:
                    use(None, u)
                for j in range(L.ahead):
                    norm(Group(0), 0, j)

            def head(g, h):
                for j in range(4):
                    if L.step(g, h, j, L.ahead):
                        norm(*L.step(g, h, j, L.ahead))
                    if j == 0 and L.rope and L.step(g, h, 0, 4):
                        q_sum(*L.step(g, h, 0, 4)[:2])
                    for u in L.slot_uses(g, h, j):
                        if u[0] != "out":
                            use(g, u)
                    for kind, wg, piece in w_jobs(L, g, h, j):
                        w_low(kind, wg, piece)

            walk(pool, L, prologue, head, lambda g: None)

        def xn_tile(t, c):
            return [z[:, c, t * P:(t + 1) * P] for z in (xnT_hi, xnT_lo)]

        def add_row(dve, layer, bump):
            for t in range(NT):
                ins = dve.scalar_tensor_tensor(x_sb[:, t, :], rows[:, :], gates[:, 4 + layer:5 + layer],
                                               x_sb[:, t, :], ALU.mult, ALU.add)
            after(dve, ins)

        def add_tiles(dve, layer, banks, ready):
            for t in range(NT):
                dve.wait_ge(ready, t + 1)
                ins = dve.scalar_tensor_tensor(x_sb[:, t, :], banks[t], gates[:, 4 + layer:5 + layer],
                                               x_sb[:, t, :], ALU.mult, ALU.add)
            after(dve, ins)
            dve.sem_inc(x_ready, 1)

        f0_banks = [psX[:, 0, :], psX[:, 1, :], psS[:, 0, :], psS[:, 1, :]]

        def f0_sync(sp):
            sp.wait_ge(x_ready, 2)
            sp.dma_start(wo_f[:, :, :], a["f0_wT"]).then_inc(f0_dma, 16)
            for i, z in enumerate(("bias", "scale", "ln_gamma", "ln_beta")):
                sp.dma_start(p_sb[:, i * D:(i + 1) * D], a[f"L0_ffn_{z}"].partition_broadcast(P)).then_inc(f0_dma, 16)
            sp.dma_start(vecs[:, 0:1], a["L0_ffn_quant_scale"].partition_broadcast(P)).then_inc(f0_dma, 16)

        def f0_tensor(pe):
            pe.wait_ge(ln_lo, 2 * NT)
            pe.wait_ge(f0_w, 1)
            for t in range(NT):
                for c in range(DC):
                    hi, lo = xn_tile(t, c)
                    pe.matmul(f0_banks[t], hi, wo_hi[:, c, :], start=(c == 0), stop=False)
                    mm = pe.matmul(f0_banks[t], lo, wo_hi[:, c, :], start=False, stop=(c == DC - 1))
                mm.then_inc(f0_mm, 1)

        def f0_vector(dve):
            dve.wait_ge(f0_dma, 16 * 6)
            after(dve, dve.tensor_scalar(wo_lo[:, :, :], wo_f[:, :, :], 0.1, None, ALU.is_ge))
            dve.scalar_tensor_tensor(wo_hi[:, :, :], wo_f[:, :, :], -0.1, wo_lo[:, :, :].bitcast(F32),
                                     ALU.is_le, ALU.subtract, reverse1=True).then_inc(f0_w, 1)
            dve.wait_ge(f0_w, 1)
            dve.reciprocal(vecs[:, 1:2], vecs[:, 0:1])
            bias, scale, gamma, beta = (p_sb[:, i * D:(i + 1) * D] for i in range(4))
            y = [wo_f[:, t, :] for t in range(NT)]
            for t in range(NT):
                dve.wait_ge(f0_mm, t + 1)
                ins = dve.tensor_tensor(y[t], f0_banks[t], bias, ALU.add)
            after(dve, ins)
            for t in range(NT):
                ins = dve.tensor_tensor(y[t], y[t], scale, ALU.mult)
            after(dve, ins)
            for t in range(NT):
                ins = dve.bn_stats(ln_stat[:, t, :], y[t])
            after(dve, ins)
            for t in range(NT):
                ins = dve.bn_aggr(ln_mv[:, t, :], ln_stat[:, t, :])
            after(dve, ins)
            dve.tensor_scalar(ln_var[:, :], ln_mv[:, :, 1], EPS, None, ALU.add).then_inc(f0_var, 1)
            dve.wait_ge(f0_pow, 1)
            for t in range(NT):
                ins = dve.tensor_scalar(y[t], y[t], ln_mv[:, t, 0:1], ln_rstd[:, t:t + 1], ALU.subtract, ALU.mult)
            after(dve, ins)
            for t in range(NT):
                ins = dve.tensor_tensor(y[t], y[t], gamma, ALU.mult)
            after(dve, ins)
            for t in range(NT):
                dve.tensor_tensor(y[t], y[t], beta, ALU.add).then_inc(f0_y, 1)
            for t in range(NT):
                dve.wait_ge(f0_tanh, t + 1)
                ins = dve.tensor_scalar(y[t], y[t], 127.0, ROUND, ALU.mult, ALU.add)
            after(dve, ins)
            for t in range(NT):
                ins = dve.tensor_scalar(y[t], y[t], -ROUND, 1.0 / 127.0, ALU.add, ALU.mult)
            after(dve, ins)
            add_tiles(dve, 0, y, f0_tanh)

        def f0_gpsimd(pool):
            pool.wait_ge(f0_var, 1)
            pool.tensor_tensor(ln_rstd[:, :], ln_var[:, :], half[:, :], ALU.pow).then_inc(f0_pow, 1)

        def f0_scalar(act):
            for t in range(NT):
                act.wait_ge(f0_y, t + 1)
                act.activation(wo_f[:, t, :], wo_f[:, t, :], ACT.Tanh, scale=vecs[:, 1:2]).then_inc(f0_tanh, 1)

        f1_banks = [psT[:, 0, :], psT[:, 1, :], psX[:, 0, :], psX[:, 1, :]]
        f1_rows = [min(P, H1 - c * P) for c in range(H1C)]

        def f1_sync(sp):
            sp.wait_ge(x_ready, 4)
            for par in (0, 1):
                sp.wait_ge(dq_out[par], 16 * ((DQ_PIECES + 1 - par) // 2))
            sp.dma_start(vecs[:, 0:H1C], a["f1_b_up"]).then_inc(f1_vec, 16)
            sp.dma_start(rows[:, :], a["L1_ffn_b_down"].partition_broadcast(P)).then_inc(f1_vec, 16)
            for c, n in enumerate(f1_rows):
                if c >= 2:
                    sp.wait_ge(f1_lo, c - 1)
                sp.dma_start(wq_f[:, c % 2, 0:DC * n].rearrange("p (c n) -> p c n", c=DC),
                             scratch_up[:, :, c * P:c * P + n].rearrange("c p n -> p c n")).then_inc(f1_dma[c % 2], 16)
                sp.dma_start(wkv_f[0:n, c % 2, :], scratch_down[c * P:c * P + n, :]).then_inc(f1_dma[c % 2], 16)

        def f1_tensor(pe):
            pe.wait_ge(ln_lo, 4 * NT)

            def up(c):
                n = f1_rows[c]
                pe.wait_ge(f1_lo, c + 1)
                if c >= 2:
                    pe.wait_ge(f1_relu, c - 1)
                three(pe, psS[0:n, c % 2, :], [([z[:, c % 2, m * n:(m + 1) * n] for z in (wq_hi, wq_lo)],
                                                (xnT_hi[:, m, :], xnT_lo[:, m, :])) for m in range(DC)]).then_inc(f1_up, 1)

            up(0)
            for c, n in enumerate(f1_rows):
                if c + 1 < H1C:
                    up(c + 1)
                pe.wait_ge(f1_ylo, c + 1)
                for t in range(NT):
                    mm = three(pe, f1_banks[t], [([z[0:n, c % 2, t * P:(t + 1) * P] for z in (q_hi, q_lo)],
                                                  [z[0:n, c % 2, :] for z in (wkv_hi, wkv_lo)])],
                               first=(c == 0), last=(c == H1C - 1))
                mm.then_inc(f1_down, 1)

        def f1_vector(dve):
            dve.wait_ge(f1_vec, 32)
            add_row(dve, 1, 0)

            def high(c):
                n = f1_rows[c]
                dve.wait_ge(f1_dma[c % 2], 32 * (c // 2 + 1))
                if c >= 2:
                    dve.wait_ge(f1_down, c - 1)
                dve.tensor_copy(wq_hi[:, c % 2, 0:DC * n], wq_f[:, c % 2, 0:DC * n])
                dve.tensor_copy(wkv_hi[0:n, c % 2, :], wkv_f[0:n, c % 2, :]).then_inc(f1_hi, 1)

            high(0)
            high(1)
            for c, n in enumerate(f1_rows):
                dve.wait_ge(f1_yhi, c + 1)
                dve.tensor_tensor(q_lo[0:n, c % 2, :], qscr[0:n, c % 2, :], q_hi[0:n, c % 2, :].bitcast(F32),
                                  ALU.subtract).then_inc(f1_ylo, 1)
                if c + 2 < H1C:
                    high(c + 2)
            dve.wait_ge(f1_down, H1C)
            for t in range(NT):
                ins = dve.scalar_tensor_tensor(x_sb[:, t, :], f1_banks[t], gates[:, 5:6], x_sb[:, t, :],
                                               ALU.mult, ALU.add)
            after(dve, ins)
            dve.sem_inc(x_ready, 1)

        def f1_gpsimd(pool):
            for c, n in enumerate(f1_rows):
                pool.wait_ge(f1_hi, c + 1)
                pool.tensor_tensor(wq_lo[:, c % 2, 0:DC * n], wq_f[:, c % 2, 0:DC * n],
                                   wq_hi[:, c % 2, 0:DC * n].bitcast(F32), ALU.subtract)
                pool.tensor_tensor(wkv_lo[0:n, c % 2, :], wkv_f[0:n, c % 2, :],
                                   wkv_hi[0:n, c % 2, :].bitcast(F32), ALU.subtract).then_inc(f1_lo, 1)

        def f1_scalar(act):
            act.wait_ge(f1_vec, 32)
            for c, n in enumerate(f1_rows):
                act.wait_ge(f1_up, c + 1)
                act.activation(qscr[0:n, c % 2, :], psS[0:n, c % 2, :], ACT.Relu,
                               bias=vecs[0:n, c:c + 1]).then_inc(f1_relu, 1)
                act.wait_ge(f1_relu, c + 1)
                if c >= 2:
                    act.wait_ge(f1_down, c - 1)
                act.activation(q_hi[0:n, c % 2, :], qscr[0:n, c % 2, :], ACT.Copy).then_inc(f1_yhi, 1)

        AR = NE * RANK + NE
        f2_h_banks = [psS[:, 0, :], psS[:, 1, :], psT[:, 0, :], psT[:, 1, :]]
        f2_out_banks = [psX[:, 0, :], psX[:, 1, :], psQ[:, :], psS[:, 0, :]]
        ar_f, ar_hi, ar_lo = (z[:, :, :].rearrange("p a b -> p (a b)")[:, 0:DC * AR] for z in (wkv_f, wkv_hi, wkv_lo))

        def f2_sync(sp):
            sp.wait_ge(x_ready, 6)
            sp.dma_start(ar_f, a["f2_ar"]).then_inc(f2_dma, 16)
            sp.dma_start(vecs[:, 0:NE * NE], a["c_before"].partition_broadcast(P)).then_inc(f2_dma, 16)
            sp.dma_start(wo_f[:, :, :], a["f2_wT"]).then_inc(f2_dma, 16)
            sp.dma_start(wq_f[:, 0, :], a["f2_b"]).then_inc(f2_dma, 16)
            sp.dma_start(rows[:, :], a["L2_ffn_b_base"].partition_broadcast(P)).then_inc(f2_dma, 16)

        def f2_tensor(pe):
            pe.wait_ge(ln_lo, 6 * NT)
            pe.wait_ge(f2_ar, 1)
            for t in range(NT):
                three(pe, f2_h_banks[t][:, 0:AR], [(xn_tile(t, c), [z[:, c * AR:(c + 1) * AR] for z in (ar_hi, ar_lo)])
                                                   for c in range(DC)]).then_inc(f2_h, 1)
            pe.wait_ge(f2_hw, 1)
            for t in range(NT):
                mm = pe.transpose(psO[:, t * P:(t + 1) * P], flat(scr[:, :, :])[:, t * P:(t + 1) * P],
                                  ident[:, :])
            mm.then_inc(f2_tp, 1)
            pe.wait_ge(f2_hwlo, 1)
            for t in range(NT):
                pairs = [(xn_tile(t, c), [z[:, c, :] for z in (wo_hi, wo_lo)]) for c in range(DC)]
                pairs.append(([z[:, 0, t * P:(t + 1) * P] for z in (q_hi, q_lo)], [z[:, 0, :] for z in (wq_hi, wq_lo)]))
                three(pe, f2_out_banks[t], pairs).then_inc(f2_out, 1)

        def f2_vector(dve):
            dve.wait_ge(f2_dma, 16 * 5)
            after(dve, dve.tensor_copy(ar_hi, ar_f))
            dve.tensor_tensor(ar_lo, ar_f, ar_hi.bitcast(F32), ALU.subtract).then_inc(f2_ar, 1)
            dve.tensor_copy(wo_hi[:, :, :], wo_f[:, :, :])
            after(dve, dve.tensor_copy(wq_hi[:, 0, :], wq_f[:, 0, :]))
            dve.tensor_tensor(wo_lo[:, :, :], wo_f[:, :, :], wo_hi[:, :, :].bitcast(F32), ALU.subtract)
            dve.tensor_tensor(wq_lo[:, 0, :], wq_f[:, 0, :], wq_hi[:, 0, :].bitcast(F32), ALU.subtract)
            add_row(dve, 2, 0)
            lg, ex, pr, rank, w = (moe[:, i, :].rearrange("p (t e) -> p t e", e=NE) for i in range(5))
            mx, sm, rc = (moe[:, 5 + i, 0:NT] for i in range(3))
            gt, eq = (ksq[:, i, 0:NT * NE * NE].rearrange("p (t e f) -> p t e f", e=NE, f=NE) for i in range(2))
            gt3, eq3 = (z.rearrange("p t e f -> p t (e f)") for z in (gt, eq))

            def wide(z):
                return z.unsqueeze(2).broadcast_to([P, NT, NE])

            for t in range(NT):
                dve.wait_ge(f2_h, t + 1)
                ins = dve.tensor_copy(lg[:, t, :], f2_h_banks[t][:, NE * RANK:AR])
            after(dve, ins)
            after(dve, dve.tensor_reduce(mx, lg, AX.X, ALU.max))
            dve.tensor_tensor(lg, lg, wide(mx), ALU.subtract).then_inc(f2_lg, 1)
            dve.wait_ge(f2_exp, 1)
            after(dve, dve.tensor_reduce(sm, ex, AX.X, ALU.add))
            after(dve, dve.reciprocal(rc, sm))
            after(dve, dve.tensor_tensor(pr, ex, wide(rc), ALU.mult))
            pf = pr.unsqueeze(2).broadcast_to([P, NT, NE, NE])
            pe_ = pr.unsqueeze(3).broadcast_to([P, NT, NE, NE])
            dve.tensor_tensor(gt, pf, pe_, ALU.is_gt)
            after(dve, dve.tensor_tensor(eq, pf, pe_, ALU.is_equal))
            before = vecs[:, 0:NE * NE].unsqueeze(1).broadcast_to([P, NT, NE * NE])
            after(dve, dve.tensor_tensor(eq3, eq3, before, ALU.mult))
            after(dve, dve.tensor_tensor(gt3, gt3, eq3, ALU.add))
            after(dve, dve.tensor_reduce(rank, gt, AX.X, ALU.add))
            after(dve, dve.scalar_tensor_tensor(w, rank, 2.0, pr, ALU.is_lt, ALU.mult))
            after(dve, dve.tensor_reduce(sm, w, AX.X, ALU.add))
            after(dve, dve.reciprocal(rc, sm))
            after(dve, dve.scalar_tensor_tensor(w, w, 2.0, wide(rc), ALU.mult, ALU.mult))
            for t in range(NT):
                hw = flat(scr[:, :, :])[:, t * P:(t + 1) * P].rearrange("p (e r) -> p e r", r=RANK)
                ins = dve.tensor_tensor(hw, f2_h_banks[t][:, 0:NE * RANK].rearrange("p (e r) -> p e r", r=RANK),
                                        w[:, t, :].unsqueeze(2).broadcast_to([P, NE, RANK]), ALU.mult)
            ins.then_inc(f2_hw, 1)
            dve.wait_ge(f2_hwhi, 1)
            dve.tensor_tensor(q_lo[:, 0, :], psO[:, :], q_hi[:, 0, :].bitcast(F32), ALU.subtract).then_inc(f2_hwlo, 1)
            add_tiles(dve, 2, f2_out_banks, f2_out)

        def f2_scalar(act):
            act.wait_ge(f2_lg, 1)
            act.activation(moe[:, 1, :], moe[:, 0, :], ACT.Exp).then_inc(f2_exp, 1)
            act.wait_ge(f2_tp, 1)
            act.activation(q_hi[:, 0, :], psO[:, :], ACT.Copy).then_inc(f2_hwhi, 1)

        f3_ab_banks = [psS[:, 0, :], psS[:, 1, :], psO[:, :], psQ[:, :]]
        f3_out_banks = [psX[:, 0, :], psX[:, 1, :], psT[:, 0, :], psT[:, 1, :]]

        def f3_sync(sp):
            sp.wait_ge(x_ready, 8)
            sp.dma_start(wo_f[:, :, :], a["f3_wT"]).then_inc(f3_dma, 16)
            sp.dma_start(wq_f[0:RANK, 0, :], a["L3_ffn_B"]).then_inc(f3_dma, 16)
            sp.dma_start(wq_f[0:RANK, 1, :], a["f3_aT"]).then_inc(f3_dma, 16)
            sp.dma_start(rows[:, :], a["L3_ffn_bias"].partition_broadcast(P)).then_inc(f3_dma, 16)

        def f3_tensor(pe):
            pe.wait_ge(f3_dma, 64)
            for c in range(DC):
                pe.matmul(f3_ab_banks[c], wq_f[0:RANK, 0, c * P:(c + 1) * P], wq_f[0:RANK, 1, :],
                          start=True, stop=True).then_inc(f3_ab, 1)

        def f3_tensor_out(pe):
            pe.wait_ge(ln_lo, 8 * NT)
            pe.wait_ge(f3_w, 1)
            for t in range(NT):
                three(pe, f3_out_banks[t], [(xn_tile(t, c), [z[:, c, :] for z in (wo_hi, wo_lo)])
                                            for c in range(DC)]).then_inc(f3_out, 1)

        def f3_vector(dve):
            dve.wait_ge(f3_dma, 64)
            add_row(dve, 3, 0)
            for c in range(DC):
                dve.wait_ge(f3_ab, c + 1)
                ins = dve.scalar_tensor_tensor(wo_f[:, c, :], f3_ab_banks[c], 1.0 / RANK, wo_f[:, c, :],
                                               ALU.mult, ALU.add)
            after(dve, ins)
            after(dve, dve.tensor_copy(wo_hi[:, :, :], wo_f[:, :, :]))
            dve.tensor_tensor(wo_lo[:, :, :], wo_f[:, :, :], wo_hi[:, :, :].bitcast(F32), ALU.subtract).then_inc(f3_w, 1)
            add_tiles(dve, 3, f3_out_banks, f3_out)

        block = ctx.enter_context(nc.Block())

        @block.sync
        def _(sp):
            start_sync(sp)
            dq_sync(sp)
            for L, ffn in zip(layers, (f0_sync, f1_sync, f2_sync, f3_sync)):
                attn_sync(sp, L)
                ffn(sp)
            sp.wait_ge(x_ready, 9)
            sp.dma_start(out.rearrange("b (t p) d -> p (b t) d", p=P), x_sb[:, :, :]).then_inc(out_dma, 16)
            sp.wait_ge(out_dma, 16)

        @block.tensor
        def _(pe):
            dq_tensor(pe)
            for L, ffn in zip(layers, (f0_tensor, f1_tensor, f2_tensor, f3_tensor_out)):
                ln_tensor(pe, 2 * L.i)
                pe.wait_ge(ln_lo, NT * (2 * L.i + 1))
                attn_tensor(pe, L)
                ln_tensor(pe, 2 * L.i + 1)
                if L.i == 3:
                    f3_tensor(pe)
                ffn(pe)

        @block.vector
        def _(dve):
            start_vector(dve)
            dq_vector(dve)
            dve.wait_ge(dq_done, DQ_PIECES + 2)
            dve.sem_inc(x_ready, 1)
            for L, ffn in zip(layers, (f0_vector, f1_vector, f2_vector, f3_vector)):
                ln_vector(dve, 2 * L.i)
                attn_vector(dve, L)
                ln_vector(dve, 2 * L.i + 1)
                ffn(dve)

        @block.scalar
        def _(act):
            start_scalar(act)
            dq_scalar(act)
            for L, ffn in zip(layers, (f0_scalar, f1_scalar, f2_scalar, lambda act: None)):
                ln_scalar(act, 2 * L.i)
                attn_scalar(act, L)
                ln_scalar(act, 2 * L.i + 1)
                ffn(act)

        @block.gpsimd
        def _(pool):
            dq_gpsimd(pool)
            for L, ffn in zip(layers, (f0_gpsimd, f1_gpsimd, lambda pool: None, lambda pool: None)):
                ln_gpsimd(pool, 2 * L.i)
                attn_gpsimd(pool, L)
                ln_gpsimd(pool, 2 * L.i + 1)
                ffn(pool)


def kernel(**inputs):
    import numpy as np
    import concourse.bacc as bacc
    from concourse.bass_utils import run_bass_kernel_spmd

    z = {k: np.asarray(v) for k, v in inputs.items()}

    def split(w, parts):
        d, n = w.shape
        return w.reshape(d // P, P, parts, n // parts).transpose(2, 1, 0, 3)

    def cols(w):
        return w.reshape(DC, P, -1).transpose(1, 0, 2)

    def attn(i, wq, wk, wv, wo, n, hd):
        arrays[f"a{i}_wq"] = split(wq, n * G4).reshape(n * G4, P, DC * hd)
        k, v = (split(w, n).reshape(n, P, DC * hd) for w in (wk, wv))
        arrays[f"a{i}_wkv"] = np.stack([k, v], axis=2)
        arrays[f"a{i}_wo"] = wo.reshape(n, G4, hd, D).transpose(0, 2, 1, 3)

    arrays = {"x": z["x"], "ctxT": cols(z["ctx_4096"].reshape(B * CTX, D).T),
              "g_xattn": z["g_xattn"], "g_ffn": z["g_ffn"]}
    arrays["c_ident"] = np.eye(P, dtype=np.float32)
    arrays["c_ones"] = np.ones((P, P), np.float32)
    hd = 128
    inv_freq = (np.float32(1.0) / np.float32(10000.0) ** (np.arange(0, hd, 2, dtype=np.float32) / np.float32(hd))).astype(np.float32)
    ang = (np.arange(SQ, dtype=np.float32)[:, None] * inv_freq[None, :]).astype(np.float32)
    cos, sin = np.cos(ang).T, np.sin(ang).T
    cos, sin = np.concatenate([cos, cos]), np.concatenate([sin, -sin])
    causal = np.where(np.arange(SQ)[:, None] >= np.arange(SQ)[None, :], 0.0, NEG).astype(np.float32)
    arrays["c_causal_trig"] = np.concatenate([causal.reshape(2, P, SQ).transpose(1, 0, 2).reshape(P, 2 * SQ), cos, sin],
                                             axis=1).astype(np.float32)
    arrays["c_before"] = (np.arange(NE)[None, :] < np.arange(NE)[:, None]).astype(np.float32).reshape(-1)

    wkv = z["L0_xattn_Wkv"]
    attn(0, z["L0_xattn_Wq"], wkv[:, :1024], wkv[:, 1024:], z["L0_xattn_Wo"], 8, 128)
    attn(1, z["L1_xattn_Wq"].T, z["L1_xattn_Wk"].T, z["L1_xattn_Wv"].T, z["L1_xattn_Wd"].T, 8, 128)
    attn(2, z["L2_xattn_Wq"].T, z["L2_xattn_Wk"].T, z["L2_xattn_Wv"].T, z["L2_xattn_Wo"].T, 4, 96)
    attn(3, z["L3_xattn_Wq"].T, z["L3_xattn_Wk"].T, z["L3_xattn_Wv"].T, z["L3_xattn_Wo"].T, 8, 128)
    arrays["a0_vecs"] = np.concatenate([z["L0_xattn_bq"].reshape(32, P), z["L0_xattn_bkv"].reshape(16, P)]).T
    arrays["a3_vecs"] = np.stack([z["L3_xattn_q_norm_w"], z["L3_xattn_k_norm_w"]], axis=1)
    arrays["a3_mask"] = z["mask_1x1xSxS2_ff0"].reshape(2, P, CTX).transpose(1, 0, 2).reshape(P, 2 * CTX)
    arrays["L0_xattn_bo"] = z["L0_xattn_bo"]
    arrays["f0_wT"] = cols(z["L0_ffn_weight"].T)
    for k in ("bias", "scale", "ln_gamma", "ln_beta", "quant_scale"):
        arrays[f"L0_ffn_{k}"] = z[f"L0_ffn_{k}"]
    up, down = (z[f"L1_ffn_w_{k}_codes"] for k in ("up", "down"))
    arrays["codes_up"] = up.reshape(H1, D).T.reshape(DC, P, H1)
    arrays["codes_down"] = down.reshape(D, H1).T
    up, down = (np.repeat(z[f"L1_ffn_w_{k}_absmax"], 64) for k in ("up", "down"))
    arrays["amax_up"] = up.reshape(H1, D).T.reshape(DC, P, H1)
    arrays["amax_down"] = down.reshape(D, H1).T
    arrays["lora_l_up"], arrays["lora_r_up"] = z["L1_ffn_w_up_lora_a"].T, z["L1_ffn_w_up_lora_b"]
    arrays["lora_l_down"], arrays["lora_r_down"] = z["L1_ffn_w_down_lora_a"].T, z["L1_ffn_w_down_lora_b"]
    arrays["f1_b_up"] = np.concatenate([z["L1_ffn_b_up"], np.zeros(H1C * P - H1, np.float32)]).reshape(H1C, P).T
    arrays["L1_ffn_b_down"] = z["L1_ffn_b_down"]
    arrays["f2_ar"] = cols(np.concatenate([z["L2_ffn_A"].reshape(NE * RANK, D), z["L2_ffn_W_router"]]).T).reshape(P, -1)
    arrays["f2_wT"] = cols(z["L2_ffn_W_base"].T)
    arrays["f2_b"] = z["L2_ffn_B"].transpose(0, 2, 1).reshape(NE * RANK, D)
    arrays["L2_ffn_b_base"] = z["L2_ffn_b_base"]
    arrays["f3_wT"] = cols(z["L3_ffn_W_q"].T)
    arrays["L3_ffn_B"] = z["L3_ffn_B"]
    arrays["f3_aT"] = z["L3_ffn_A"].T
    arrays["L3_ffn_bias"] = z["L3_ffn_bias"]

    nc = bacc.Bacc("TRN2", target_bir_lowering=False, num_devices=1, dynamic_dma_scratch_size=1024)
    a, feed = {}, {}
    for name, v in arrays.items():
        v = np.ascontiguousarray(v)
        feed["in_" + name] = v
        a[name] = nc.dram_tensor("in_" + name, v.shape, mybir.dt.from_np(v.dtype), kind="ExternalInput").ap()
    for i in range(4):
        a[f"attn{i}"] = {k: a[f"a{i}_{k}"] for k in ("wq", "wkv", "wo", "vecs", "mask") if f"a{i}_{k}" in a}
    a["attn1"]["mask"] = a["c_causal_trig"]
    out = nc.dram_tensor("out", (B, SQ, D), F32, kind="ExternalOutput").ap()
    scratch_up = nc.dram_tensor("w_up", (DC, P, H1), F32).ap()
    scratch_down = nc.dram_tensor("w_down", (H1, D), F32).ap()
    program(nc, a, out, scratch_up, scratch_down)
    r = run_bass_kernel_spmd(nc, [feed], core_ids=[0])
    return r.results[0]["out"]
```

```python
from contextlib import ExitStack

import concourse.bass as bass
from concourse import mybir

F32 = mybir.dt.float32
F32R = mybir.dt.float32r
I32 = mybir.dt.int32
ALU = mybir.AluOpType
ACT = mybir.ActivationFunctionType
AX = mybir.AxisListType

P = 128
B = 2
SQ = 256
TOK = B * SQ
D = 512
DC = D // P
NT = TOK // P
CTX = 512
G4 = 4
EPS = 1e-5
NEG = -1e30
H1 = 1376
H1C = -(-H1 // P)
NE, RANK = 8, 16
NF4 = [-1.0, -0.6961928009986877, -0.5250730514526367, -0.39491748809814453, -0.28444138169288635,
       -0.18477343022823334, -0.09105003625154495, 0.0, 0.07958029955625534, 0.16093020141124725,
       0.24611230194568634, 0.33791524171829224, 0.44070982933044434, 0.5626170039176941,
       0.7229568362236023, 1.0]
H1_LAST = H1 - (H1C - 1) * P
W1_COLS = (H1C - 1) * 2 * D + DC * H1_LAST + D
DQ = W1_COLS // 32
assert DQ * 32 == W1_COLS
ROUND = 1.5 * 2.0 ** 23

ATTN = [
    dict(kind="bias", hd=128, groups=8, keys=512, nbuf=2, ahead=2, q_slot=1,
         prep={(1, 0): ["k0"], (1, 3): ["k1"], (2, 0): ["v0"], (2, 3): ["v1"], (3, 0): ["t0"], (3, 2): ["t1"]}),
    dict(kind="rope", hd=128, groups=8, keys=256, nbuf=2, ahead=2, q_slot=1,
         prep={(1, 3): ["k0"], (2, 3): ["v0"], (3, 3): ["t0"]}),
    dict(kind="plain", hd=96, groups=4, keys=768, nbuf=1, ahead=1, q_slot=3,
         prep={(1, 0): ["k0"], (1, 1): ["k1"], (1, 2): ["k2"], (2, 0): ["v0"], (2, 1): ["v1"], (2, 2): ["t0"],
               (3, 0): ["v2"], (3, 1): ["t1"], (3, 2): ["t2"]}),
    dict(kind="rms", hd=128, groups=8, keys=512, nbuf=2, ahead=2, q_slot=1,
         prep={(1, 0): ["k0"], (1, 2): ["k1", "m0"], (1, 3): ["m1", "b0"], (2, 0): ["b1"],
               (2, 3): ["v0"], (3, 0): ["t0"], (3, 2): ["v1"], (3, 3): ["t1"]}),
]


COUNTERS = ("wqA_dma wqB_dma wkv_dma wo_dma vec_dma wq_hi wq_lo wkv_hi wkv_lo wo_hi wo_lo "
            "q_mm q_hi q_lo q_f q_sum q_r s_mm s_nm s_mask s_max s_exp s_rec s_norm t_mm t_hi t_lo "
            "av_mm o_hi o_lo x_mm x_act x_free k_f k_hi k_lo k_r k_diag").split()


class Group:

    def __init__(self, off, loop=None, last=False, mul=2):
        self.off, self.loop, self.last, self.mul = off, loop, last, mul
        self.par = off % 2

    def at(self, per_group, const):
        assert self.loop is None or per_group * self.off + const > 0
        return self.address(per_group, const)

    def address(self, per_group, const):
        if self.loop is None:
            return per_group * self.off + const
        return self.loop * (self.mul * per_group) + (per_group * self.off + const)

    def half(self, per_two, const):
        value = per_two * (self.off // 2) + const
        return value if self.loop is None else self.loop * (self.mul // 2 * per_two) + value

    def to(self, d, last=False):
        return Group(self.off + d, self.loop, last)


class Counter:

    def __init__(self, sem, base=0):
        self.sem, self.base = sem, base

    def wait(self, eng, value):
        if isinstance(value, int) and value <= 0:
            return
        eng.wait_ge(self.sem, value + self.base)

    def inc(self, ins, by=1):
        ins.then_inc(self.sem, by)


class Layer:

    def __init__(self, index, sems):
        cfg = ATTN[index]
        self.i, self.kind, self.hd, self.n = index, cfg["kind"], cfg["hd"], cfg["groups"]
        self.keys, self.nbuf, self.ahead, self.prep = cfg["keys"], cfg["nbuf"], cfg["ahead"], cfg["prep"]
        self.kt, self.q_slot = self.keys // P, cfg["q_slot"]
        self.scale = float(self.hd) ** -0.5
        self.rms, self.rope = self.kind == "rms", self.kind == "rope"
        self.masked = self.rms or self.rope
        self.flat = [u for slot in self.prep.values() for u in slot]
        every = [u for h in range(G4) for j in range(4) for u in self.plan(h, j)]
        prepared = set(self.flat)
        self.order = {u: i for i, u in enumerate(every)}
        self.last_order = {u: i for i, u in enumerate(
            [u for u in every if u not in prepared and u != ("q", G4 - 1)])}
        self.first_order = {u: i for i, u in enumerate([u for u in every if u[0] != "out"])}
        self.first = self.flat + ([("q", -1)] if self.rms else [])
        self.n_vec = dict(bias=16, rope=16, plain=0, rms=32)[self.kind]
        self.n_k = len([u for u in self.flat if u[0] == "k"])
        n = self.n
        self.total_x = len(self.first) - 4 + len(self.order) * (n - 1) + len(self.last_order) + 4
        act_uses = len([u for u in self.flat if u[0] in ("t" if self.masked else "kt")])
        total = dict(wqA_dma=32 * n, wqB_dma=32 * n, wkv_dma=16 * n, wo_dma=16 * n, vec_dma=self.n_vec,
                     wq_hi=4 * n, wq_lo=4 * n, wkv_hi=2 * n, wkv_lo=2 * n, wo_hi=4 * n, wo_lo=4 * n,
                     q_mm=4 * n, q_hi=4 * n, q_lo=4 * n, s_mm=16 * n, s_nm=0 if self.masked else 16 * n,
                     s_max=16 * n, s_exp=16 * n, s_rec=16 * n, s_norm=16 * n, t_mm=16 * n, t_hi=16 * n,
                     t_lo=16 * n, av_mm=8 * n, o_hi=4 * n, o_lo=4 * n, x_mm=self.total_x,
                     x_free=self.total_x, x_act=act_uses * n, s_mask=16 * n if self.masked else 0,
                     k_f=self.n_k * n if self.masked else 0, k_hi=self.n_k * n if self.masked else 0,
                     k_lo=self.n_k * n if self.masked else 0, q_f=4 * n if self.masked else 0,
                     q_sum=4 * n if self.rope else 0, q_r=4 * n if self.rms else 0,
                     k_r=2 * n if self.rms else 0, k_diag=2 * n if self.rms else 0)
        counters = [Counter(sems[name][0], sems[name][1]) for name in COUNTERS]
        (wqA_dma, wqB_dma, self.wkv_dma, self.wo_dma, self.vec_dma, self.wq_hi, self.wq_lo, self.wkv_hi,
         self.wkv_lo, self.wo_hi, self.wo_lo, self.q_mm, self.q_hi, self.q_lo, self.q_f, self.q_sum,
         self.q_r, self.s_mm, self.s_nm, self.s_mask, self.s_max, self.s_exp, self.s_rec, self.s_norm,
         self.t_mm, self.t_hi, self.t_lo, self.av_mm, self.o_hi, self.o_lo, self.x_mm, self.x_act,
         self.x_free, self.k_f, self.k_hi, self.k_lo, self.k_r, self.k_diag) = counters
        self.wq_dma = (wqA_dma, wqB_dma)
        for name in COUNTERS:
            sems[name] = (sems[name][0], sems[name][1] + total[name])

    def use(self, g, what):
        if g is None:
            k = self.first.index(what)
            return k, k % 2
        if what[0] == "end":
            k = self.total_x - 4 + what[1]
            return k, k % 2
        if g.loop is None and g.off == 0:
            k = len(self.first) + self.first_order[what]
            return k, k % 2
        order = self.last_order if g.last else self.order
        c = len(self.first) - 4 + order[what]
        return g.at(len(self.order), c), (c + len(self.order) * g.par) % 2

    def plan(self, h, j):
        out = [("out", t) for t in ([], [0], [1], [2, 3])[j]] if h == 0 else []
        if self.rms and j == 1:
            out.append(("q", h))
        return out + self.prep.get((h, j), [])

    def slot_uses(self, g, h, j):
        order = self.last_order if g.last else self.order
        first = g.loop is None and g.off == 0
        return [u for u in self.plan(h, j) if u in order and not (first and u[0] == "out")]

    def open(self, j):
        return P if self.rope and j % 2 == 0 else self.keys

    def count(self, g, letters, what):
        mine = [u for u in self.flat if u[0] in letters]
        at = mine.index(what) + 1
        return at if g is None else g.at(len(mine), len(mine) + at)

    def step(self, g, h, j, d):
        k = 4 * h + j + d
        if k >= 16:
            return None if g.last else (g.to(1), (k - 16) // 4, k % 4)
        return g, k // 4, k % 4


def walk(eng, L, prologue, head, tail):
    prologue()
    head(Group(0), 0)
    pairs = (L.n - 2) // 2
    with eng.Fori(0, pairs) as i:
        for d in (0, 1):
            g = Group(d, i)
            for h in (1, 2, 3):
                head(g, h)
            head(g.to(1), 0)
    g = Group(L.n - 2)
    for h in (1, 2, 3):
        head(g, h)
    g = Group(L.n - 1, last=True)
    for h in range(G4):
        head(g, h)
    tail(g)


def program(nc, a, out, scratch):
    ctx = ExitStack()
    with ctx:
        def sb(name, shape, dt=F32):
            return ctx.enter_context(nc.sbuf_tensor(name, shape, dt))

        def pb(name, shape):
            return ctx.enter_context(nc.psum_tensor(name, shape, F32))

        def sem(name):
            return ctx.enter_context(nc.semaphore(name))

        x_sb = sb("x_sb", [P, NT, D])
        xnT_hi, xnT_lo = (sb(f"xnT_{z}", [P, DC, TOK], F32R) for z in ("hi", "lo"))
        cT_hi, cT_lo = (sb(f"cT_{z}", [P, DC, B * CTX], F32R) for z in ("hi", "lo"))
        ident = sb("ident", [P, P])
        ones = sb("ones", [P, P])
        gates = sb("gates", [P, 8])
        half = sb("half", [P, 4])
        ln_stat = sb("ln_stat", [P, NT, 6])
        ln_mv = sb("ln_mv", [P, NT, 2])
        ln_var = sb("ln_var", [P, NT])
        ln_rstd = sb("ln_rstd", [P, NT])
        xn_f = sb("xn_f", [P, 2, D])
        rows = sb("rows", [P, D])
        kT_hi, kT_lo = (sb(f"kT_{z}", [P, 2, B * CTX], F32R) for z in ("hi", "lo"))
        with nc.sbuf_tensor("dq_space", [P, 4, CTX], F32) as dq_space:
            pass
        kx_hi, kx_lo = (sb(f"kx_{z}", [P, 2, CTX], F32R) for z in ("hi", "lo"))
        v_hi, v_lo = (sb(f"v_{z}", [P, 2, 12 * 96], F32R) for z in ("hi", "lo"))
        wq_f = sb("wq_f", [P, 2, DC * P])
        wq_hi, wq_lo = (sb(f"wq_{z}", [P, 2, DC * P], F32R) for z in ("hi", "lo"))
        wkv_f = sb("wkv_f", [P, 2, DC * P])
        wkv_hi, wkv_lo = (sb(f"wkv_{z}", [P, 2, DC * P], F32R) for z in ("hi", "lo"))
        wo_f = sb("wo_f", [P, G4, D])
        wo_hi, wo_lo = (sb(f"wo_{z}", [P, G4, D], F32R) for z in ("hi", "lo"))
        oT_hi, oT_lo = (sb(f"oT_{z}", [P, G4, TOK], F32R) for z in ("hi", "lo"))
        q_hi, q_lo = (sb(f"q_{z}", [P, 2, TOK], F32R) for z in ("hi", "lo"))
        p_sb = sb("p_sb", [P, 2048])
        pT_hi, pT_lo = (sb(f"pT_{z}", [P, 2, 6 * SQ], F32R) for z in ("hi", "lo"))
        scr = sb("scr", [P, 2, 512])
        qscr = sb("qscr", [P, 2, TOK])
        ksq = xn_f
        mask_sb = sb("mask_sb", [P, 2 * CTX])
        trig = mask_sb[:, 2 * SQ:4 * SQ].rearrange("p (z m) -> p z m", z=2)
        vecs = sb("vecs", [P, 64])
        nmax, nbias, rsum, rrec = (sb(z, [P, 4]) for z in ("nmax", "nbias", "rsum", "rrec"))
        q_ms, q_r, k_ms, k_r = (sb(z, [P, 2, 4]) for z in ("q_ms", "q_r", "k_ms", "k_r"))
        diag = rows[:, :].rearrange("p (a b) -> p a b", b=P)
        moe = xn_f[:, 0, 256:512].rearrange("p (i n) -> p i n", n=NT * NE)

        psS = pb("psS", [P, 2, 512])
        psT = pb("psT", [P, 2, 512])
        psO = pb("psO", [P, 512])
        psQ = pb("psQ", [P, 512])
        psX = pb("psX", [P, 2, 512])

        const_dma, gate_dma, gate_done, half_done = (sem(z) for z in
                                                     ("const_dma", "gate_dma", "gate_done", "half_done"))
        ctx_dma, ctx_lo = [sem("ctxA_dma"), sem("ctxB_dma")], sem("ctx_lo")
        ctx_hi = sem("ctx_hi")
        wait_met = sem("wait_met")
        dve_self = sem("dve_self")
        x_ready = sem("x_ready")
        ln_stats, ln_pow, ln_xn, ln_tp, ln_hi, ln_lo = (sem(z) for z in
                                                        ("ln_stats", "ln_pow", "ln_xn", "ln_tp", "ln_hi", "ln_lo"))
        row_dma, out_dma = sem("row_dma"), sem("out_dma")
        dq_code = [sem("dq_codeA_dma"), sem("dq_codeB_dma")]
        dq_amax, dq_out, dq_bits, dq_leafA, dq_leafB, dq_pair, dq_low, dq_high, dq_sel, dq_done = (
            sem(f"dq_{z}") for z in ("amax_dma", "out", "bits", "leafA", "leafB", "pair", "low", "high", "sel", "done"))
        f0_dma, f0_w, f0_mm, f0_var, f0_pow, f0_y, f0_tanh = (
            sem(f"f0_{z}") for z in ("dma", "w", "mm", "var", "pow", "y", "tanh"))
        f1_vec, f1_hi, f1_lo, f1_up, f1_relu, f1_yhi, f1_ylo, f1_down = (
            sem(f"f1_{z}") for z in ("vec", "hi", "lo", "up", "relu", "yhi", "ylo", "down"))
        f1_lsplit, f1_lmm, f1_lhi, f1_llo = (sem(f"f1_{z}") for z in ("lsplit", "lmm", "lhi", "llo"))
        f1_dma, f1_ddma = ([sem(f"f1_{z}A_dma"), sem(f"f1_{z}B_dma")] for z in ("up", "down"))
        f1_dhi, f1_dlo = sem("f1_dhi"), sem("f1_dlo")
        f2_dma, f2_ar, f2_h, f2_lg, f2_exp, f2_hw, f2_tp, f2_hwhi, f2_hwlo, f2_out = (
            sem(f"f2_{z}") for z in ("dma", "ar", "h", "lg", "exp", "hw", "tp", "hwhi", "hwlo", "out"))
        f3_dma, f3_ab, f3_w, f3_out = (sem(f"f3_{z}") for z in ("dma", "ab", "w", "out"))
        sems = {name: (sem(name), 0) for name in COUNTERS}
        layers = [Layer(i, sems) for i in range(4)]
        own = [0]

        def after(dve, ins):
            own[0] += 1
            ins.then_inc(dve_self, 1)
            dve.wait_ge(dve_self, own[0])

        def three(pe, dst, pairs, first=True, last=True):
            n, k = 3 * len(pairs), 0
            for (wh, wl), (mh, ml) in pairs:
                for w, m in ((wh, mh), (wl, mh), (wh, ml)):
                    mm = pe.matmul(dst, w, m, start=(first and k == 0), stop=(last and k == n - 1))
                    k += 1
            return mm

        def start_sync(sp):
            sp.dma_start(ident[:, :], a["c_ident"]).then_inc(const_dma, 16)
            sp.dma_start(ones[:, :], a["c_ones"]).then_inc(const_dma, 16)
            sp.dma_start(x_sb[:, :, :], a["x"].rearrange("b (t p) d -> p (b t) d", p=P)).then_inc(const_dma, 16)
            sp.dma_start(gates[:, 0:4], a["g_xattn"].partition_broadcast(P)).then_inc(gate_dma, 16)
            sp.dma_start(gates[:, 4:8], a["g_ffn"].partition_broadcast(P)).then_inc(gate_dma, 16)
            for c in range(DC):
                if c >= 2:
                    sp.wait_ge(ctx_lo, c - 1)
                sp.dma_start(p_sb[:, (c % 2) * 1024:(c % 2 + 1) * 1024],
                             a["ctxT"][:, c, :]).then_inc(ctx_dma[c % 2], 16)

        def start_vector(dve):
            dve.memset(half[:, :], -0.5).then_inc(half_done, 1)
            for c in range(DC):
                dve.wait_ge(ctx_dma[c % 2], 16 * (c // 2 + 1))
                f = p_sb[:, (c % 2) * 1024:(c % 2 + 1) * 1024]
                dve.tensor_copy(cT_hi[:, c, :], f).then_inc(ctx_hi, 1)
                dve.wait_ge(ctx_hi, c + 1)
                dve.tensor_tensor(cT_lo[:, c, :], f, cT_hi[:, c, :].bitcast(F32), ALU.subtract).then_inc(ctx_lo, 1)
            dve.wait_ge(ctx_lo, DC)

        def start_scalar(act):
            act.wait_ge(gate_dma, 32)
            act.activation(gates[:, :], gates[:, :], ACT.Tanh).then_inc(gate_done, 1)

        spare = [dq_space[:, i, 0:DQ] for i in range(4)]
        dq_codes = [mask_sb[:, i * DQ:(i + 1) * DQ].bitcast(I32) for i in (0, 1)]
        dq_bit = [xn_f[:, 0, 0:DQ].bitcast(I32), xn_f[:, 1, 0:DQ].bitcast(I32), rows[:, 0:DQ].bitcast(I32)]
        dq_w = qscr[:, 1, 0:DQ]
        leaf = {0: [qscr[:, 0, 0:DQ], spare[0], spare[1], spare[2]], 8: [spare[3], spare[0], spare[1], spare[2]]}

        def dq_sync(sp, g, h):
            if g is not None and (h or g.off or g.loop is not None):
                sp.wait_ge(dq_done, g.at(4, h))
                sp.dma_start(scratch[:, bass.ds(g.address(4 * DQ, (h - 1) * DQ), DQ)], dq_w).then_inc(dq_out, 16)
            if g is None:
                sp.dma_start(dq_codes[0], a["codes"][:, 0:DQ]).then_inc(dq_code[0], 16)
                return
            if not (g.last and h == 3):
                sp.dma_start(dq_codes[(h + 1) % 2],
                             a["codes"][:, bass.ds(g.address(4 * DQ, (h + 1) * DQ), DQ)]).then_inc(dq_code[(h + 1) % 2], 16)
            if h or g.off or g.loop is not None:
                sp.wait_ge(dq_out, g.at(64, 16 * h))
                sp.dma_start(dq_w, a["amax"][:, bass.ds(g.address(4 * DQ, h * DQ), DQ)]).then_inc(dq_amax, 16)
            else:
                sp.dma_start(dq_w, a["amax"][:, 0:DQ]).then_inc(dq_amax, 16)

        def dq_sync_end(sp):
            sp.wait_ge(dq_done, 32)
            sp.dma_start(scratch[:, 31 * DQ:32 * DQ], dq_w).then_inc(dq_out, 16)

        def dq_scalar(act, g, h, j):
            k = g.at(4, h + 1)
            first = g.loop is None and g.off == 0 and h == 0
            if j == 0:
                act.wait_ge(dq_bits, k)
                if not first:
                    act.wait_ge(dq_done, g.at(4, h))
            elif j == 2:
                act.wait_ge(dq_low, k)
            else:
                return
            side, ready = (0, dq_leafA) if j == 0 else (8, dq_leafB)
            for q in range(4):
                lo, hi = NF4[side + 2 * q], NF4[side + 2 * q + 1]
                ins = act.activation(leaf[side][q], dq_bit[0], ACT.Copy, scale=hi - lo, bias=lo)
            ins.then_inc(ready, 1)

        def dq_select(dve, to, bit, other, wait_for, value):
            dve.wait_ge(wait_for, value)
            dve.sem_inc(wait_met, 1)
            return dve.copy_predicated(to, bit, other)

        def dq_vector(dve, g, h, stage):
            k = g.at(4, h + 1)
            first = g.loop is None and g.off == 0 and h == 0
            codes, (bit0, bit1, bit2) = dq_codes[h % 2], dq_bit
            low, high = leaf[0], leaf[8]
            if stage == "bits":
                dve.wait_ge(dq_code[h % 2], g.at(32, 16 * (h // 2 + 1)))
                if not first:
                    dve.wait_ge(dq_sel, g.at(4, h))
                for i, bit in enumerate(dq_bit):
                    dve.tensor_scalar(bit, codes, 1 << i, None, ALU.bitwise_and)
                dve.tensor_scalar(codes, codes, 8, None, ALU.bitwise_and).then_inc(dq_bits, 1)
            elif stage == "low pairs":
                dq_select(dve, low[0], bit1, low[1], dq_leafA, k)
                dve.copy_predicated(low[2], bit1, low[3]).then_inc(dq_pair, 1)
            elif stage == "low":
                dq_select(dve, low[0], bit2, low[2], dq_pair, g.at(8, 2 * h + 1)).then_inc(dq_low, 1)
            elif stage == "high pairs":
                dq_select(dve, high[0], bit1, high[1], dq_leafB, k)
                dve.copy_predicated(high[2], bit1, high[3]).then_inc(dq_pair, 1)
            elif stage == "high":
                dq_select(dve, high[0], bit2, high[2], dq_pair, g.at(8, 2 * h + 2)).then_inc(dq_high, 1)
            else:
                dq_select(dve, low[0], codes, high[0], dq_high, k).then_inc(dq_sel, 1)

        def dq_gpsimd(pool, g, h):
            pool.wait_ge(dq_amax, g.at(64, 16 * (h + 1)))
            pool.wait_ge(dq_sel, g.at(4, h + 1))
            pool.tensor_tensor(dq_w, leaf[0][0], dq_w, ALU.mult).then_inc(dq_done, 1)

        ln_banks = [psT[:, 0, :], psT[:, 1, :], psS[:, 0, :], psS[:, 1, :]]

        def ln_tile_stats(dve, k, t):
            after(dve, dve.bn_stats(ln_stat[:, t, :], x_sb[:, t, :]))
            after(dve, dve.bn_aggr(ln_mv[:, t, :], ln_stat[:, t, :]))
            dve.tensor_scalar(ln_var[:, t:t + 1], ln_mv[:, t, 1:2], EPS, None, ALU.add).then_inc(ln_stats, 1)

        def ln_tile(dve, k, t):
            dve.wait_ge(ln_pow, NT * k + t + 1)
            if t >= 2 or k >= 1:
                dve.wait_ge(ln_tp, NT * k + t - 1)
            dve.tensor_scalar(xn_f[:, t % 2, :], x_sb[:, t, :], ln_mv[:, t, 0:1], ln_rstd[:, t:t + 1],
                              ALU.subtract, ALU.mult).then_inc(ln_xn, 1)

        def finish(dve, k, add):
            for t in range(NT):
                add(t)
                if k < 8:
                    ln_tile_stats(dve, k, t)
                    if t >= 1:
                        ln_tile(dve, k, t - 1)
            dve.sem_inc(x_ready, 1)
            if k == 8:
                return

            def low(t):
                dve.wait_ge(ln_hi, NT * k + t + 1)
                cols = slice(t * P, (t + 1) * P)
                dve.tensor_tensor(xnT_lo[:, :, cols], ln_banks[t].rearrange("p (c n) -> p c n", c=DC),
                                  xnT_hi[:, :, cols].bitcast(F32), ALU.subtract).then_inc(ln_lo, 1)

            low(0)
            ln_tile(dve, k, NT - 1)
            for t in range(1, NT):
                low(t)

        def ln_gpsimd(pool, k):
            if k == 0:
                pool.wait_ge(half_done, 1)
            for t in range(NT):
                pool.wait_ge(ln_stats, NT * k + t + 1)
                pool.tensor_tensor(ln_rstd[:, t:t + 1], ln_var[:, t:t + 1], half[:, 0:1], ALU.pow).then_inc(ln_pow, 1)

        def ln_tensor(pe, k):
            if k == 0:
                pe.wait_ge(const_dma, 48)
            for t in range(NT):
                pe.wait_ge(ln_xn, NT * k + t + 1)
                for c in range(DC):
                    mm = pe.transpose(ln_banks[t][:, c * P:(c + 1) * P], xn_f[:, t % 2, c * P:(c + 1) * P],
                                      ident[:, :])
                mm.then_inc(ln_tp, 1)

        def ln_scalar(act, k):
            for t in range(NT):
                act.wait_ge(ln_tp, NT * k + t + 1)
                act.activation(xnT_hi[:, :, t * P:(t + 1) * P],
                               ln_banks[t].rearrange("p (c n) -> p c n", c=DC),
                               ACT.Copy).then_inc(ln_hi, 1)

        def flat(t):
            return t.rearrange("p a b -> p (a b)")

        def s_view(L, j):
            return flat(psS[:, :, :])[:, 0:L.keys] if L.nbuf == 1 else psS[:, j % 2, 0:L.keys]

        def t_view(L, j):
            v = flat(psT[:, :, :])[:, 0:L.keys] if L.nbuf == 1 else psT[:, j % 2, 0:L.open(j)]
            return v.rearrange("p (m q) -> p m q", q=P)

        def p_view(L, j):
            at = (j % 2) * 768 if L.nbuf == 1 else j * 512
            return p_sb[:, at:at + L.open(j)]

        def pT_view(L, z, j):
            b, t = j // 2, j % 2
            v = z[:, b, 0:L.kt * SQ].rearrange("p (m q) -> p m q", q=SQ)
            return v[:, 0:L.open(j) // P, t * P:(t + 1) * P]

        def k_cols(par, col, n):
            if col >= B * CTX:
                return [z[:, par, col - B * CTX:col - B * CTX + n] for z in (kx_hi, kx_lo)]
            return [z[:, par, col:col + n] for z in (kT_hi, kT_lo)]

        def w_jobs(L, g, h, j):
            out = []
            if j == 3 and not (g.last and h >= 1):
                out.append(("wq", (g.to(1) if h >= 1 else g), (h + 3) % 4))
            if h == 0 and j in (0, 2) and not g.last:
                out.append(("wkv", g.to(1), j // 2))
            if h in (1, 2) and j in (0, 2):
                out.append(("wo", g, 2 * (h - 1) + j // 2))
            return out

        def w_parts(L, kind, piece):
            n = DC * L.hd
            if kind == "wq":
                return [z[:, piece % 2, 0:n] for z in (wq_f, wq_hi, wq_lo)]
            if kind == "wkv":
                return [z[:, piece, 0:n] for z in (wkv_f, wkv_hi, wkv_lo)]
            return [z[0:L.hd, piece, :] for z in (wo_f, wo_hi, wo_lo)]

        def attn_sync(sp, L):
            names = a[f"attn{L.i}"]

            def load_wq(g, h):
                k = g.at(4, h)
                L.wq_lo.wait(sp, g.at(4, h - 1))
                n = DC * L.hd
                L.wq_dma[h % 2].inc(
                    sp.dma_start(wq_f[:, h % 2, 0:n], names["wq"][k, :, :]), 16)

            def load_wkv(g):
                L.wkv_lo.wait(sp, g.at(2, 0))
                L.wkv_dma.inc(sp.dma_start(wkv_f[:, :, 0:DC * L.hd], names["wkv"][g.at(1, 0), :, :, :]), 16)

            def load_wo(g):
                L.wo_lo.wait(sp, g.at(4, 0))
                L.wo_dma.inc(sp.dma_start(wo_f[0:L.hd, :, :], names["wo"][g.at(1, 0), :, :, :]), 16)

            sp.wait_ge(x_ready, 2 * L.i + 1)
            load_wkv(Group(0))
            load_wq(Group(0), 0)
            load_wq(Group(0), 1)
            load_wq(Group(0), 2)
            if "vecs" in names:
                L.vec_dma.inc(sp.dma_start(vecs[:, 0:names["vecs"].shape[1]], names["vecs"]), 16)
            if L.masked:
                L.vec_dma.inc(sp.dma_start(mask_sb[:, 0:names["mask"].shape[1]], names["mask"]), 16)
            if L.i == 0:
                sp.dma_start(rows[:, :], a["L0_xattn_bo"].partition_broadcast(P)).then_inc(row_dma, 16)
                dq_sync(sp, None, 0)

            def head(g, h):
                if not (g.last and h >= 1):
                    load_wq(g.to(1) if h >= 1 else g, (h + 3) % 4)
                if h == 0 and not g.last:
                    load_wkv(g.to(1))
                if h == 0:
                    load_wo(g)
                if L.i == 0:
                    dq_sync(sp, g, h)

            walk(sp, L, lambda: None, head, lambda g: None)
            if L.i == 0:
                dq_sync_end(sp)

        def attn_tensor(pe, L):
            hd = L.hd

            def q_proj(g, h):
                L.wq_lo.wait(pe, g.at(4, h + 1))
                (L.q_f if L.rope else L.q_lo).wait(pe, g.at(4, h) if g.off or g.loop is not None or h else 0)
                L.q_mm.inc(three(pe, psQ[0:hd, :], [
                    ([z[:, h % 2, c * hd:(c + 1) * hd] for z in (wq_hi, wq_lo)],
                     (xnT_hi[:, c, :], xnT_lo[:, c, :])) for c in range(DC)]))

            def scores(g, h, j):
                b, t = j // 2, j % 2
                if j == 0:
                    L.q_lo.wait(pe, g.at(4, h + 1))
                    if h == 0:
                        if L.masked:
                            L.k_lo.wait(pe, g.at(L.n_k, L.n_k))
                        else:
                            prev = g.to(-1) if g.off else None
                            L.x_free.wait(pe, L.use(prev, f"k{L.n_k - 1}")[0] + 1)
                free = L.s_mask if L.masked else L.s_exp
                free.wait(pe, g.at(16, 4 * h + j - L.nbuf + 1))
                q = [z[0:hd, h % 2, b * SQ + t * P:b * SQ + (t + 1) * P] for z in (q_hi, q_lo)]
                if L.kind == "plain":
                    parts = [(b * CTX, CTX, 0), (2 * CTX + b * SQ, SQ, CTX)]
                else:
                    parts = [(b * L.keys, L.keys, 0)]
                for col, n, to in parts:
                    mm = three(pe, s_view(L, j)[:, to:to + n],
                               [(q, [z[0:hd] for z in k_cols(g.par, col, n)])])
                L.s_mm.inc(mm)

            def transposes(g, h, j):
                L.s_norm.wait(pe, g.at(16, 4 * h + j + 1))
                L.t_lo.wait(pe, g.at(16, 4 * h + j - L.nbuf + 1) if (g.off or g.loop is not None or h or j >= L.nbuf)
                            else 0)
                for m in range(L.open(j) // P):
                    mm = pe.transpose(t_view(L, j)[:, m, :], p_view(L, j)[:, m * P:(m + 1) * P], ident[:, :])
                L.t_mm.inc(mm)

            def weighted_v(g, h, b):
                L.t_lo.wait(pe, g.at(16, 4 * h + 2 * b + 2))
                if b == 0:
                    L.o_lo.wait(pe, g.at(4, h) if g.off or g.loop is not None or h else 0)
                    if h == 0:
                        prev = g.to(-1) if g.off else None
                        L.x_free.wait(pe, L.use(prev, L.flat[-1])[0] + 1)
                pairs = []
                for m in range(L.kt):
                    if L.kind == "plain":
                        tile = 4 * b + m if m < 4 else 8 + 2 * b + (m - 4)
                    else:
                        tile = L.kt * b + m
                    pairs.append(([z[:, g.par, tile * hd:(tile + 1) * hd] for z in (v_hi, v_lo)],
                                  [z[:, b, m * SQ:(m + 1) * SQ] for z in (pT_hi, pT_lo)]))
                L.av_mm.inc(three(pe, psO[0:hd, b * SQ:(b + 1) * SQ], pairs))

            def use(g, what, gp):
                k, bank = L.use(g, what)
                if not (isinstance(k, int) and k < 2):
                    L.x_free.wait(pe, k - 1)
                X = psX[:, bank, :]
                kind, i = what[0], int(what[1])
                if kind in ("out", "end"):
                    L.o_lo.wait(pe, gp.at(4, 4))
                    L.wo_lo.wait(pe, gp.at(4, 4))
                    mm = three(pe, X, [([z[0:hd, h, i * P:(i + 1) * P] for z in (oT_hi, oT_lo)],
                                        [z[0:hd, h, :] for z in (wo_hi, wo_lo)]) for h in range(G4)])
                elif kind in "kv":
                    L.wkv_lo.wait(pe, gp.at(2, 1 if kind == "k" else 2))
                    pairs = []
                    for c in range(DC):
                        w = [z[:, int(kind == "v"), c * hd:(c + 1) * hd] for z in (wkv_hi, wkv_lo)]
                        if L.rope:
                            m = [z[:, c, :].rearrange("p (b m) -> p b m", b=B)[:, :, 0:L.keys] for z in (cT_hi, cT_lo)]
                        elif i == 2:
                            m = [z[:, c, :] for z in (xnT_hi, xnT_lo)]
                        else:
                            m = [z[:, c, i * CTX:(i + 1) * CTX] for z in (cT_hi, cT_lo)]
                        pairs.append((w, m))
                    dst = X[0:hd, :].rearrange("p (b m) -> p b m", b=B) if L.rope else X[0:hd, :]
                    mm = three(pe, dst, pairs)
                elif kind == "t":
                    L.x_free.wait(pe, L.use(g, f"v{i}")[0] + 1)
                    for m in range(4):
                        mm = pe.transpose(X[:, m * hd:(m + 1) * hd], scr[0:hd, i % 2, m * P:(m + 1) * P],
                                          ident[0:hd, 0:hd])
                elif kind == "m":
                    L.k_f.wait(pe, L.count(g, "k", f"k{i}"))
                    for m in range(4):
                        mm = pe.matmul(X[:, m:m + 1], ksq[:, i, m * P:(m + 1) * P], ones[:, 0:1],
                                       start=True, stop=True)
                elif kind == "b":
                    L.k_diag.wait(pe, L.count(g, "b", what))
                    mm = pe.matmul(X, ones[:, :], diag[:, :, :].rearrange("p a b -> p (a b)"), start=True, stop=True)
                else:
                    h = what[1] + 1
                    L.q_f.wait(pe, (Group(0) if g is None else g).at(4, h + 1))
                    for m in range(4):
                        mm = pe.matmul(X[:, m:m + 1], qscr[:, h % 2, m * P:(m + 1) * P], ones[:, 0:1],
                                       start=True, stop=True)
                L.x_mm.inc(mm)

            def prologue():
                q_proj(Group(0), 0)
                for u in L.first:
                    use(None, u, Group(0))
                q_proj(Group(0), 1)
                for j in range(L.ahead):
                    scores(Group(0), 0, j)

            def head(g, h):
                for j in range(4):
                    nxt = L.step(g, h, j, L.ahead)
                    if nxt:
                        scores(*nxt)
                    transposes(g, h, j)
                    if j == 0 and (h or g.off or g.loop is not None):
                        weighted_v(*((g, h - 1) if h else (g.to(-1), 3)), 1)
                    if j == 2:
                        weighted_v(g, h, 0)
                    for u in L.slot_uses(g, h, j):
                        use(g, u, g.to(-1) if u[0] == "out" else g.to(1))
                    if j == L.q_slot and L.step(g, h, 0, 8):
                        q_proj(*L.step(g, h, 0, 8)[:2])

            def tail(g):
                weighted_v(g, 3, 1)
                for t in range(NT):
                    use(g, ("end", t), g)

            walk(pe, L, prologue, head, tail)

        def rotated(dve, src, dst):
            h = P // 2
            src = src.rearrange("p (b m) -> p b m", b=B)
            cos, sin = (trig[:, i, :].unsqueeze(1).broadcast_to([P, B, SQ]) for i in (0, 1))
            by_cos, by_sin = (dst[:, i, :].rearrange("p (b m) -> p b m", b=B) for i in (0, 1))
            dve.tensor_tensor(by_cos, src, cos, ALU.mult)
            dve.tensor_tensor(by_sin[0:h], src[h:P], sin[h:P], ALU.mult)
            return dve.tensor_tensor(by_sin[h:P], src[0:h], sin[0:h], ALU.mult)

        def attn_vector(dve, L):
            hd = L.hd
            gate = gates[:, L.i:L.i + 1]
            late = []

            def row_max(g, h, j):
                k = 4 * h + j
                L.s_mm.wait(dve, g.at(16, k + 1))
                if L.masked:
                    if L.rms and j == 0:
                        L.q_r.wait(dve, g.at(4, h + 1))
                    scale = q_r[:, h % 2, j:j + 1] if L.rms else L.scale
                    t = j % 2
                    L.s_mask.inc(dve.scalar_tensor_tensor(p_view(L, j), s_view(L, j)[:, 0:L.open(j)], scale,
                                                          mask_sb[:, t * L.keys:t * L.keys + L.open(j)],
                                                          ALU.mult, ALU.add))
                    L.s_mask.wait(dve, g.at(16, k + 1))
                    L.s_max.inc(dve.tensor_reduce(nbias[:, j:j + 1], p_view(L, j), AX.X, ALU.max, negate=True))
                else:
                    L.s_nm.inc(dve.tensor_reduce(nmax[:, j:j + 1], s_view(L, j), AX.X, ALU.max, negate=True))
                    L.s_nm.wait(dve, g.at(16, k + 1))
                    L.s_max.inc(dve.tensor_scalar(nbias[:, j:j + 1], nmax[:, j:j + 1], L.scale, None, ALU.mult))

            def row_recip(g, h, j):
                L.s_exp.wait(dve, g.at(16, 4 * h + j + 1))
                L.s_rec.inc(dve.reciprocal(rrec[:, j:j + 1], rsum[:, j:j + 1]))

            def pT_low(g, h, j):
                L.t_hi.wait(dve, g.at(16, 4 * h + j + 1))
                L.t_lo.inc(dve.tensor_tensor(pT_view(L, pT_lo, j), t_view(L, j), pT_view(L, pT_hi, j).bitcast(F32),
                                             ALU.subtract))

            def q_front(g, h):
                L.q_mm.wait(dve, g.at(4, h + 1))
                L.q_f.inc(rotated(dve, psQ[:, :], qscr))

            def q_low(g, h):
                L.q_hi.wait(dve, g.at(4, h + 1))
                lo, hi, src = q_lo[0:hd, h % 2, :], q_hi[0:hd, h % 2, :].bitcast(F32), psQ[0:hd, :]
                if L.kind == "bias":
                    col = g.at(4, h) if g.off or g.loop is not None or h else 0
                    ins = dve.scalar_tensor_tensor(lo, src, vecs[:, bass.ds(col, 1)], hi, ALU.add, ALU.subtract)
                elif L.rms:
                    ins = dve.scalar_tensor_tensor(lo, src, vecs[:, 0:1], hi, ALU.mult, ALU.subtract)
                else:
                    ins = dve.tensor_tensor(lo, qscr[:, 0, :] if L.rope else src, hi, ALU.subtract)
                L.q_lo.inc(ins)

            def o_low(g, h):
                L.o_hi.wait(dve, g.at(4, h + 1))
                L.o_lo.inc(dve.tensor_tensor(oT_lo[0:hd, h, :], psO[0:hd, :], oT_hi[0:hd, h, :].bitcast(F32),
                                             ALU.subtract))

            def k_low(g, i, kpar):
                L.k_hi.wait(dve, L.count(g, "k", f"k{i}"))
                k_hi, k_lo = k_cols(kpar, i * CTX, CTX)
                L.k_lo.inc(dve.tensor_tensor(k_lo, scr[:, i, :], k_hi.bitcast(F32), ALU.subtract))

            def use(g, what, gp):
                k, bank = L.use(g, what)
                X = psX[:, bank, :]
                kind, i = what[0], int(what[1])
                kpar = gp.par
                if kind == "k":
                    k_hi, k_lo = k_cols(kpar, i * CTX, CTX)
                act_letters = "t" if L.masked else "kt"
                if kind == "t" or (kind == "k" and not L.masked):
                    L.x_act.wait(dve, L.count(g, act_letters, what))
                elif kind == "k" and L.rms:
                    L.k_f.wait(dve, L.count(g, "k", what))
                else:
                    L.x_mm.wait(dve, k + 1)
                if kind == "v" and L.masked:
                    L.k_lo.wait(dve, L.count(g, "k", f"k{i}"))
                if kind in ("out", "end"):
                    ins = dve.scalar_tensor_tensor(x_sb[:, i, :], X, gate, x_sb[:, i, :], ALU.mult, ALU.add)
                elif kind == "k" and L.kind == "bias":
                    bk = vecs[:, bass.ds(gp.at(1, 4 * L.n), 1)]
                    ins = dve.scalar_tensor_tensor(k_lo, X, bk, k_hi.bitcast(F32), ALU.add, ALU.subtract)
                elif kind == "k" and L.kind == "plain":
                    ins = dve.tensor_tensor(k_lo[0:hd], X[0:hd, :], k_hi[0:hd].bitcast(F32), ALU.subtract)
                elif kind == "k" and L.rope:
                    ins = rotated(dve, X, scr)
                    late.append((g, i, kpar))
                elif kind == "k":
                    ins = dve.tensor_scalar(scr[:, i, :], X, vecs[:, 1:2], None, ALU.mult)
                elif kind == "m":
                    ins = dve.tensor_scalar(k_ms[:, i, :], X[:, 0:4], 1.0 / hd, EPS, ALU.mult, ALU.add)
                elif kind == "b":
                    ins = dve.tensor_tensor(scr[:, i, :], scr[:, i, :], X, ALU.mult)
                    late.append((g, i, kpar))
                elif kind == "v" and L.kind == "bias":
                    bv = vecs[:, bass.ds(gp.at(1, 5 * L.n), 1)]
                    ins = dve.tensor_scalar(scr[:, i % 2, :], X, bv, None, ALU.add)
                elif kind == "v":
                    ins = dve.tensor_copy(scr[0:hd, i % 2, :], X[0:hd, :])
                elif kind == "t":
                    c = slice(i * 4 * hd, (i + 1) * 4 * hd)
                    ins = dve.tensor_tensor(v_lo[:, kpar, c], X[:, 0:4 * hd], v_hi[:, kpar, c].bitcast(F32),
                                            ALU.subtract)
                else:
                    ins = dve.tensor_scalar(q_ms[:, (what[1] + 1) % 2, :], X[:, 0:4], EPS * hd, None, ALU.add)
                L.x_free.inc(ins)

            def do_late(end=B):
                while late and late[0][1] < end:
                    k_low(*late.pop(0))

            def prologue():
                L.vec_dma.wait(dve, L.n_vec)
                if L.i == 0:
                    dve.wait_ge(row_dma, 16)
                    dve.wait_ge(gate_done, 1)
                    for t in range(NT):
                        ins = dve.scalar_tensor_tensor(x_sb[:, t, :], rows[:, :], gate, x_sb[:, t, :],
                                                       ALU.mult, ALU.add)
                    after(dve, ins)
                if L.rope:
                    for z in (pT_hi, pT_lo):
                        dve.memset(z[:, :, SQ:SQ + P].bitcast(F32), 0.0)
                    q_front(Group(0), 0)
                q_low(Group(0), 0)
                for u in L.first:
                    if u[0] == "v":
                        do_late()
                    use(None, u, Group(0))
                (q_front if L.rope else q_low)(Group(0), 1)
                for j in range(L.ahead):
                    row_max(Group(0), 0, j)
                for j in range(L.ahead):
                    row_recip(Group(0), 0, j)

            def head(g, h):
                for j in range(4):
                    nxt = L.step(g, h, j, L.ahead)
                    if j == 1 and h == 0 and (g.off or g.loop is not None):
                        o_low(g.to(-1), 3)
                    if nxt:
                        row_max(*nxt)
                    pT_low(g, h, j)
                    if nxt:
                        row_recip(*nxt)
                    if j == 1 and h:
                        o_low(g, h - 1)
                    if j == 0 and L.rope and L.step(g, h, 0, 4):
                        q_low(*L.step(g, h, 0, 4)[:2])
                    if L.i == 0 and j != 2:
                        dq_vector(dve, g, h, {0: "bits", 1: "low pairs", 3: "high pairs"}[j])
                    before = list(late)
                    for u in L.slot_uses(g, h, j):
                        if u[0] == "v":
                            do_late(int(u[1]) + 1)
                        use(g, u, g.to(-1) if u[0] == "out" else g.to(1))
                    while late and late[0] in before:
                        k_low(*late.pop(0))
                    if L.i == 0 and j in (1, 3):
                        dq_vector(dve, g, h, "low" if j == 1 else "high")
                    if j == L.q_slot and L.step(g, h, 0, 8):
                        (q_front if L.rope else q_low)(*L.step(g, h, 0, 8)[:2])
                    if L.i == 0 and j == 3:
                        dq_vector(dve, g, h, "all")

            def tail(g):
                o_low(g, 3)

                def add(t):
                    use(g, ("end", t), g)
                    L.x_free.wait(dve, L.use(g, ("end", t))[0] + 1)

                finish(dve, 2 * L.i + 1, add)

            walk(dve, L, prologue, head, tail)

        def attn_scalar(act, L):
            hd = L.hd
            late = []

            def w_high(kind, g, piece):
                f, hi, lo = w_parts(L, kind, piece)
                if kind == "wq":
                    L.wq_dma[piece % 2].wait(act, g.at(32, 16 * (piece // 2 + 1)))
                    L.q_mm.wait(act, g.at(4, piece - 1) if g.off or g.loop is not None or piece > 1 else 0)
                    L.wq_hi.inc(act.activation(hi, f, ACT.Copy))
                elif kind == "wkv":
                    L.wkv_dma.wait(act, g.at(16, 16))
                    L.wkv_hi.inc(act.activation(hi, f, ACT.Copy))
                else:
                    L.wo_dma.wait(act, g.at(16, 16))
                    L.wo_hi.inc(act.activation(hi, f, ACT.Copy))

            def row_exp(g, h, j):
                L.s_max.wait(act, g.at(16, 4 * h + j + 1))
                src = p_view(L, j) if L.masked else s_view(L, j)
                L.s_exp.inc(act.activation(p_view(L, j), src, ACT.Exp, bias=nbias[:, j:j + 1],
                                           scale=1.0 if L.masked else L.scale, accum_out=rsum[:, j:j + 1]))

            def pT_high(g, h, j):
                L.t_mm.wait(act, g.at(16, 4 * h + j + 1))
                L.av_mm.wait(act, g.at(8, 2 * h + j // 2 - 1) if g.off or g.loop is not None or h else 0)
                L.t_hi.inc(act.activation(pT_view(L, pT_hi, j), t_view(L, j), ACT.Copy))

            def q_high(g, h):
                dst = q_hi[0:hd, h % 2, :]
                if L.rope:
                    L.q_sum.wait(act, g.at(4, h + 1))
                    ins = act.activation(dst, qscr[:, 0, :], ACT.Copy)
                else:
                    L.q_mm.wait(act, g.at(4, h + 1))
                    if L.rms:
                        L.q_f.inc(act.activation(qscr[:, h % 2, :], psQ[:, :], ACT.Square))
                        ins = act.activation(dst, psQ[:, :], ACT.Copy, scale=vecs[:, 0:1])
                    elif L.kind == "bias":
                        col = g.at(4, h) if g.off or g.loop is not None or h else 0
                        act.sem_inc(wait_met, 1)
                        ins = act.activation(dst, psQ[:, :], ACT.Identity, bias=vecs[:, bass.ds(col, 1)])
                    else:
                        ins = act.activation(dst, psQ[0:hd, :], ACT.Copy)
                L.q_hi.inc(ins)

            def o_high(g, h):
                L.av_mm.wait(act, g.at(8, 2 * h + 2))
                if h == 0 and (g.off or g.loop is not None):
                    L.x_mm.wait(act, L.use(g, ("out", 3))[0] + 1)
                L.o_hi.inc(act.activation(oT_hi[0:hd, h, :], psO[0:hd, :], ACT.Copy))

            def use(g, what, gp):
                k, bank = L.use(g, what)
                X = psX[:, bank, :]
                kind, i = what[0], int(what[1])
                if kind in "kb":
                    k_hi = k_cols(gp.par, i * CTX, CTX)[0]
                if kind == "k" and L.rms:
                    L.x_mm.wait(act, k + 1)
                    L.k_f.inc(act.activation(ksq[:, i, :], X, ACT.Square))
                elif (kind == "k" and L.rope) or kind == "b":
                    if L.rope:
                        L.k_f.wait(act, L.count(g, "k", what))
                    else:
                        L.x_free.wait(act, k + 1)
                    L.k_hi.inc(act.activation(k_hi, scr[:, i, :], ACT.Copy))
                elif kind == "k":
                    L.x_mm.wait(act, k + 1)
                    dst = k_hi[0:hd]
                    if L.kind == "bias":
                        act.sem_inc(wait_met, 1)
                        ins = act.activation(dst, X, ACT.Identity, bias=vecs[:, bass.ds(gp.at(1, 4 * L.n), 1)])
                    else:
                        ins = act.activation(dst, X[0:hd, :], ACT.Copy)
                    L.x_act.inc(ins)
                elif kind == "t":
                    L.x_mm.wait(act, k + 1)
                    L.x_act.inc(act.activation(v_hi[:, gp.par, i * 4 * hd:(i + 1) * 4 * hd], X[:, 0:4 * hd],
                                               ACT.Copy))

            def prologue():
                for kind, piece in (("wq", 0), ("wkv", 0), ("wkv", 1), ("wq", 1)):
                    w_high(kind, Group(0), piece)
                L.vec_dma.wait(act, L.n_vec)
                q_high(Group(0), 0)
                w_high("wq", Group(0), 2)
                for u in L.first:
                    use(None, u, Group(0))
                q_high(Group(0), 1)
                for j in range(L.ahead):
                    row_exp(Group(0), 0, j)

            def head(g, h):
                for j in range(4):
                    pT_high(g, h, j)
                    nxt = L.step(g, h, j, L.ahead)
                    if nxt:
                        row_exp(*nxt)
                    if j == 0 and (h or g.off or g.loop is not None):
                        o_high(*((g, h - 1) if h else (g.to(-1), 3)))
                    if j == 3 and L.rope and L.step(g, h, 0, 8):
                        q_high(*L.step(g, h, 0, 8)[:2])
                    while late:
                        use(*late.pop(0))
                    for u in L.slot_uses(g, h, j):
                        if u[0] == "b" or (u[0] == "k" and L.rope):
                            late.append((g, u, g.to(1)))
                        elif u[0] not in ("out", "q"):
                            use(g, u, g.to(1))
                    for kind, wg, piece in w_jobs(L, g, h, j):
                        w_high(kind, wg, piece)
                    if L.i == 0:
                        dq_scalar(act, g, h, j)
                    if j == L.q_slot and L.step(g, h, 0, 8) and not L.rope:
                        q_high(*L.step(g, h, 0, 8)[:2])

            walk(act, L, prologue, head, lambda g: o_high(g, 3))

        def attn_gpsimd(pool, L):
            def norm(g, h, j):
                L.s_rec.wait(pool, g.at(16, 4 * h + j + 1))
                L.s_norm.inc(pool.tensor_tensor(p_view(L, j), p_view(L, j),
                                                rrec[:, j:j + 1].broadcast_to([P, L.open(j)]), ALU.mult))

            def w_low(kind, g, piece):
                f, hi, lo = w_parts(L, kind, piece)
                if kind == "wq":
                    L.wq_hi.wait(pool, g.at(4, piece + 1))
                    L.wq_lo.inc(pool.tensor_tensor(lo, f, hi.bitcast(F32), ALU.subtract))
                elif kind == "wkv":
                    L.wkv_hi.wait(pool, g.at(2, piece + 1))
                    L.wkv_lo.inc(pool.tensor_tensor(lo, f, hi.bitcast(F32), ALU.subtract))
                else:
                    L.wo_hi.wait(pool, g.at(4, piece + 1))
                    L.wo_lo.inc(pool.tensor_tensor(lo, f, hi.bitcast(F32), ALU.subtract))

            def q_sum(g, h):
                L.q_f.wait(pool, g.at(4, h + 1))
                L.q_sum.inc(pool.tensor_tensor(qscr[:, 0, :], qscr[:, 0, :], qscr[:, 1, :], ALU.add))

            def use(g, what):
                if what[0] not in "kmq" or what[0] == "out":
                    return
                k, _ = L.use(g, what)
                if what[0] == "k" and L.rope:
                    L.x_free.wait(pool, k + 1)
                    L.k_f.inc(pool.tensor_tensor(scr[:, 0, :], scr[:, 0, :], scr[:, 1, :], ALU.add))
                elif what[0] == "m":
                    i = int(what[1])
                    L.x_free.wait(pool, k + 1)
                    L.k_r.inc(pool.tensor_tensor(k_r[:, i, :], k_ms[:, i, :], half[:, 0:4], ALU.pow))
                    L.k_r.wait(pool, L.count(g, "m", what))
                    if i:
                        L.x_mm.wait(pool, L.use(g, "b0")[0] + 1)
                    L.k_diag.inc(pool.tensor_tensor(diag[:, :, :], ident[:, :].unsqueeze(1).broadcast_to([P, 4, P]),
                                                    k_r[:, i, :].unsqueeze(2).broadcast_to([P, 4, P]), ALU.mult))
                elif what[0] == "q":
                    h = what[1] + 1
                    L.x_free.wait(pool, k + 1)
                    L.q_r.inc(pool.tensor_tensor(q_r[:, h % 2, :], q_ms[:, h % 2, :], half[:, 0:4], ALU.pow))

            def prologue():
                if L.i == 0:
                    pool.wait_ge(half_done, 1)
                for kind, piece in (("wq", 0), ("wkv", 0), ("wkv", 1), ("wq", 1)):
                    w_low(kind, Group(0), piece)
                if L.rope:
                    q_sum(Group(0), 0)
                w_low("wq", Group(0), 2)
                for u in L.first:
                    use(None, u)
                if L.rope:
                    q_sum(Group(0), 1)
                for j in range(L.ahead):
                    norm(Group(0), 0, j)

            def head(g, h):
                for j in range(4):
                    if L.step(g, h, j, L.ahead):
                        norm(*L.step(g, h, j, L.ahead))
                    if j == 2 and L.rope and L.step(g, h, 0, 8):
                        q_sum(*L.step(g, h, 0, 8)[:2])
                    for u in L.slot_uses(g, h, j):
                        if u[0] != "out":
                            use(g, u)
                    for kind, wg, piece in w_jobs(L, g, h, j):
                        w_low(kind, wg, piece)
                    if L.i == 0 and j == 3:
                        dq_gpsimd(pool, g, h)

            walk(pool, L, prologue, head, lambda g: None)

        def xn_tile(t, c):
            return [z[:, c, t * P:(t + 1) * P] for z in (xnT_hi, xnT_lo)]

        def add_row(dve, layer, bump):
            for t in range(NT):
                ins = dve.scalar_tensor_tensor(x_sb[:, t, :], rows[:, :], gates[:, 4 + layer:5 + layer],
                                               x_sb[:, t, :], ALU.mult, ALU.add)
            after(dve, ins)

        def add_tiles(dve, layer, banks, ready, base=0):
            def add(t):
                dve.wait_ge(ready, base + t + 1)
                after(dve, dve.scalar_tensor_tensor(x_sb[:, t, :], banks[t], gates[:, 4 + layer:5 + layer],
                                                    x_sb[:, t, :], ALU.mult, ALU.add))

            finish(dve, 2 * layer + 2, add)

        f0_banks = [psX[:, 0, :], psX[:, 1, :], psS[:, 0, :], psS[:, 1, :]]

        def f0_sync(sp):
            sp.wait_ge(x_ready, 2)
            sp.dma_start(wo_f[:, :, :], a["f0_wT"]).then_inc(f0_dma, 16)
            for i, z in enumerate(("bias", "scale", "ln_gamma", "ln_beta")):
                sp.dma_start(p_sb[:, i * D:(i + 1) * D], a[f"L0_ffn_{z}"].partition_broadcast(P)).then_inc(f0_dma, 16)
            sp.dma_start(vecs[:, 0:1], a["L0_ffn_quant_scale"].partition_broadcast(P)).then_inc(f0_dma, 16)

        def f0_tensor(pe):
            pe.wait_ge(f0_w, 1)
            for t in range(NT):
                pe.wait_ge(ln_lo, NT + t + 1)
                for c in range(DC):
                    hi, lo = xn_tile(t, c)
                    pe.matmul(f0_banks[t], hi, wo_hi[:, c, :], start=(c == 0), stop=False)
                    mm = pe.matmul(f0_banks[t], lo, wo_hi[:, c, :], start=False, stop=(c == DC - 1))
                mm.then_inc(f0_mm, 1)

        def f0_vector(dve):
            dve.wait_ge(f0_dma, 16 * 6)
            after(dve, dve.tensor_scalar(wo_lo[:, :, :], wo_f[:, :, :], 0.1, None, ALU.is_ge))
            dve.scalar_tensor_tensor(wo_hi[:, :, :], wo_f[:, :, :], -0.1, wo_lo[:, :, :].bitcast(F32),
                                     ALU.is_le, ALU.subtract, reverse1=True).then_inc(f0_w, 1)
            dve.wait_ge(f0_w, 1)
            dve.reciprocal(vecs[:, 1:2], vecs[:, 0:1])
            bias, scale, gamma, beta = (p_sb[:, i * D:(i + 1) * D] for i in range(4))
            y = [wo_f[:, t, :] for t in range(NT)]
            for t in range(NT):
                dve.wait_ge(f0_mm, t + 1)
                ins = dve.tensor_tensor(y[t], f0_banks[t], bias, ALU.add)
            after(dve, ins)
            for t in range(NT):
                ins = dve.tensor_tensor(y[t], y[t], scale, ALU.mult)
            after(dve, ins)
            for t in range(NT):
                ins = dve.bn_stats(ln_stat[:, t, :], y[t])
            after(dve, ins)
            for t in range(NT):
                ins = dve.bn_aggr(ln_mv[:, t, :], ln_stat[:, t, :])
            after(dve, ins)
            dve.tensor_scalar(ln_var[:, :], ln_mv[:, :, 1], EPS, None, ALU.add).then_inc(f0_var, 1)
            dve.wait_ge(f0_pow, 1)
            for t in range(NT):
                ins = dve.tensor_scalar(y[t], y[t], ln_mv[:, t, 0:1], ln_rstd[:, t:t + 1], ALU.subtract, ALU.mult)
            after(dve, ins)
            for t in range(NT):
                ins = dve.tensor_tensor(y[t], y[t], gamma, ALU.mult)
            after(dve, ins)
            for t in range(NT):
                dve.tensor_tensor(y[t], y[t], beta, ALU.add).then_inc(f0_y, 1)
            for t in range(NT):
                dve.wait_ge(f0_tanh, t + 1)
                ins = dve.tensor_scalar(y[t], y[t], 127.0, ROUND, ALU.mult, ALU.add)
            after(dve, ins)
            for t in range(NT):
                ins = dve.tensor_scalar(y[t], y[t], -ROUND, 1.0 / 127.0, ALU.add, ALU.mult)
            after(dve, ins)
            add_tiles(dve, 0, y, f0_tanh)

        def f0_gpsimd(pool):
            pool.wait_ge(f0_var, 1)
            pool.tensor_tensor(ln_rstd[:, :], ln_var[:, :], half[:, :], ALU.pow).then_inc(f0_pow, 1)

        def f0_scalar(act):
            for t in range(NT):
                act.wait_ge(f0_y, t + 1)
                act.activation(wo_f[:, t, :], wo_f[:, t, :], ACT.Tanh, scale=vecs[:, 1:2]).then_inc(f0_tanh, 1)

        f1_banks = [psT[:, 0, :], psT[:, 1, :], psX[:, 0, :], psX[:, 1, :]]
        f1_rows = [min(P, H1 - c * P) for c in range(H1C)]

        NUP, NLA = H1, DC * RANK
        la_f, la = mask_sb[:, 0:NLA + H1C * RANK], [z[:, 0, 0:NLA + H1C * RANK] for z in (oT_hi, oT_lo)]
        lb_f, lb = p_sb[0:RANK, 0:NUP + D], [flat(z[:, :, :])[0:RANK, 0:NUP + D] for z in (pT_hi, pT_lo)]
        up_l, down_l = ([z[0:RANK, i, :] for z in (oT_hi, oT_lo)] for i in (1, 2))

        def f1_sync(sp):
            sp.wait_ge(x_ready, 4)
            sp.wait_ge(dq_out, 16 * 32)
            for c in range(H1C):
                if c == 0:
                    sp.dma_start(la_f, a["f1_la"]).then_inc(f1_vec, 16)
                    sp.dma_start(lb_f, a["f1_lb"]).then_inc(f1_vec, 16)
                n = DC * f1_rows[c]
                if c >= 2:
                    sp.wait_ge(f1_lo, c - 1)
                sp.dma_start(wq_f[:, c % 2, 0:n], scratch[:, 2 * D * c:2 * D * c + n]).then_inc(f1_dma[c % 2], 16)
                if c >= 2:
                    sp.wait_ge(f1_dlo, c - 1)
                sp.dma_start(wkv_f[:, c % 2, :], scratch[:, 2 * D * c + n:2 * D * c + n + D]).then_inc(f1_ddma[c % 2], 16)
                if c == 0:
                    sp.dma_start(vecs[:, 0:H1C], a["f1_b_up"]).then_inc(f1_vec, 16)
                    sp.dma_start(rows[:, :], a["L1_ffn_b_down"].partition_broadcast(P)).then_inc(f1_vec, 16)

        def f1_tensor(pe):
            pe.wait_ge(ln_lo, 4 * NT)
            pe.wait_ge(f1_lsplit, 1)
            three(pe, psQ[0:RANK, :], [([z[:, m * RANK:(m + 1) * RANK] for z in la], (xnT_hi[:, m, :], xnT_lo[:, m, :]))
                                       for m in range(DC)]).then_inc(f1_lmm, 1)

            def up(c):
                n = f1_rows[c]
                pe.wait_ge(f1_lo, c + 1)
                if c >= 2:
                    pe.wait_ge(f1_relu, c - 1)
                three(pe, psS[0:n, c % 2, :], [([z[:, c % 2, m * n:(m + 1) * n] for z in (wq_hi, wq_lo)],
                                                (xnT_hi[:, m, :], xnT_lo[:, m, :])) for m in range(DC)], last=False)
                if c == 0:
                    pe.wait_ge(f1_llo, 1)
                three(pe, psS[0:n, c % 2, :], [([z[:, c * P:c * P + n] for z in lb], up_l)],
                      first=False).then_inc(f1_up, 1)

            up(0)
            for c, n in enumerate(f1_rows):
                if c + 1 < H1C:
                    up(c + 1)
                pe.wait_ge(f1_ylo, c + 1)
                pe.wait_ge(f1_dlo, c + 1)
                y = [z[0:n, c % 2, :] for z in (q_hi, q_lo)]
                three(pe, psO[0:RANK, :], [([z[0:n, NLA + c * RANK:NLA + (c + 1) * RANK] for z in la], y)],
                      first=(c == 0), last=(c == H1C - 1))
                for t in range(NT):
                    mm = three(pe, f1_banks[t], [([z[:, t * P:(t + 1) * P] for z in y],
                                                  [z[0:n, c % 2, :] for z in (wkv_hi, wkv_lo)])],
                               first=(c == 0), last=False)
                mm.then_inc(f1_down, 1)
            pe.wait_ge(f1_llo, 2)
            for t in range(NT):
                three(pe, f1_banks[t], [([z[:, t * P:(t + 1) * P] for z in down_l],
                                         [z[:, NUP:NUP + D] for z in lb])], first=False).then_inc(f1_down, 1)

        def f1_vector(dve):
            dve.wait_ge(f1_vec, 64)
            for f, hi in ((la_f, la[0]), (lb_f, lb[0])):
                ins = dve.tensor_copy(hi, f)
            after(dve, ins)
            for f, (hi, lo) in ((la_f, la), (lb_f, lb)):
                ins = dve.tensor_tensor(lo, f, hi.bitcast(F32), ALU.subtract)
            ins.then_inc(f1_lsplit, 1)
            add_row(dve, 1, 0)

            def low_rank(i, bank, parts):
                dve.wait_ge(f1_lhi, i + 1)
                dve.tensor_tensor(parts[1], bank, parts[0].bitcast(F32), ALU.subtract).then_inc(f1_llo, 1)

            def up_high(c):
                n = f1_rows[c]
                dve.wait_ge(f1_dma[c % 2], 16 * (c // 2 + 1))
                if c >= 2:
                    dve.wait_ge(f1_up, c - 1)
                dve.tensor_copy(wq_hi[:, c % 2, 0:DC * n], wq_f[:, c % 2, 0:DC * n]).then_inc(f1_hi, 1)

            def down_high(c):
                n = f1_rows[c]
                dve.wait_ge(f1_ddma[c % 2], 16 * (c // 2 + 1))
                if c >= 2:
                    dve.wait_ge(f1_down, c - 1)
                dve.tensor_copy(wkv_hi[0:n, c % 2, :], wkv_f[0:n, c % 2, :]).then_inc(f1_dhi, 1)

            up_high(0)
            up_high(1)
            down_high(0)
            low_rank(0, psQ[0:RANK, :], up_l)
            for c, n in enumerate(f1_rows):
                if c + 2 < H1C:
                    up_high(c + 2)
                dve.wait_ge(f1_yhi, c + 1)
                dve.tensor_tensor(q_lo[0:n, c % 2, :], qscr[0:n, c % 2, :], q_hi[0:n, c % 2, :].bitcast(F32),
                                  ALU.subtract).then_inc(f1_ylo, 1)
                if c + 1 < H1C:
                    down_high(c + 1)
            low_rank(1, psO[0:RANK, :], down_l)
            add_tiles(dve, 1, f1_banks, f1_down, base=H1C)

        def f1_gpsimd(pool):
            def up_low(c):
                n = DC * f1_rows[c]
                pool.wait_ge(f1_hi, c + 1)
                pool.tensor_tensor(wq_lo[:, c % 2, 0:n], wq_f[:, c % 2, 0:n], wq_hi[:, c % 2, 0:n].bitcast(F32),
                                   ALU.subtract).then_inc(f1_lo, 1)

            def down_low(c):
                n = f1_rows[c]
                pool.wait_ge(f1_dhi, c + 1)
                pool.tensor_tensor(wkv_lo[0:n, c % 2, :], wkv_f[0:n, c % 2, :],
                                   wkv_hi[0:n, c % 2, :].bitcast(F32), ALU.subtract).then_inc(f1_dlo, 1)

            up_low(0)
            up_low(1)
            down_low(0)
            for c in range(H1C):
                if c + 2 < H1C:
                    up_low(c + 2)
                if c + 1 < H1C:
                    down_low(c + 1)

        def f1_scalar(act):
            act.wait_ge(f1_vec, 64)
            act.wait_ge(f1_lmm, 1)
            act.activation(up_l[0], psQ[0:RANK, :], ACT.Copy).then_inc(f1_lhi, 1)
            for c, n in enumerate(f1_rows):
                act.wait_ge(f1_up, c + 1)
                act.activation(qscr[0:n, c % 2, :], psS[0:n, c % 2, :], ACT.Relu,
                               bias=vecs[0:n, c:c + 1]).then_inc(f1_relu, 1)
                act.wait_ge(f1_relu, c + 1)
                if c >= 2:
                    act.wait_ge(f1_down, c - 1)
                act.activation(q_hi[0:n, c % 2, :], qscr[0:n, c % 2, :], ACT.Copy).then_inc(f1_yhi, 1)
            act.wait_ge(f1_down, H1C)
            act.activation(down_l[0], psO[0:RANK, :], ACT.Copy).then_inc(f1_lhi, 1)

        AR = NE * RANK + NE
        f2_h_banks = ln_banks
        f2_out_banks = [psX[:, 0, :], psX[:, 1, :], psQ[:, :], psS[:, 0, :]]
        ar_f, ar_hi, ar_lo = (z[:, :, :].rearrange("p a b -> p (a b)")[:, 0:DC * AR] for z in (wkv_f, wkv_hi, wkv_lo))

        def f2_sync(sp):
            sp.wait_ge(x_ready, 6)
            sp.dma_start(ar_f, a["f2_ar"]).then_inc(f2_dma, 16)
            sp.dma_start(vecs[:, 0:NE * NE], a["c_before"].partition_broadcast(P)).then_inc(f2_dma, 16)
            sp.dma_start(wo_f[:, :, :], a["f2_wT"]).then_inc(f2_dma, 16)
            sp.dma_start(wq_f[:, 0, :], a["f2_b"]).then_inc(f2_dma, 16)
            sp.dma_start(rows[:, :], a["L2_ffn_b_base"].partition_broadcast(P)).then_inc(f2_dma, 16)

        def f2_tensor(pe):
            pe.wait_ge(f2_ar, 1)
            for t in range(NT):
                pe.wait_ge(ln_lo, 5 * NT + t + 1)
                three(pe, f2_h_banks[t][:, 0:AR], [(xn_tile(t, c), [z[:, c * AR:(c + 1) * AR] for z in (ar_hi, ar_lo)])
                                                   for c in range(DC)]).then_inc(f2_h, 1)
            pe.wait_ge(f2_hw, 1)
            for t in range(NT):
                mm = pe.transpose(psO[:, t * P:(t + 1) * P], flat(scr[:, :, :])[:, t * P:(t + 1) * P],
                                  ident[:, :])
            mm.then_inc(f2_tp, 1)
            pe.wait_ge(f2_hwlo, 1)
            for t in range(NT):
                pairs = [(xn_tile(t, c), [z[:, c, :] for z in (wo_hi, wo_lo)]) for c in range(DC)]
                pairs.append(([z[:, 0, t * P:(t + 1) * P] for z in (q_hi, q_lo)], [z[:, 0, :] for z in (wq_hi, wq_lo)]))
                three(pe, f2_out_banks[t], pairs).then_inc(f2_out, 1)

        def f2_vector(dve):
            dve.wait_ge(f2_dma, 16 * 5)
            after(dve, dve.tensor_copy(ar_hi, ar_f))
            dve.tensor_tensor(ar_lo, ar_f, ar_hi.bitcast(F32), ALU.subtract).then_inc(f2_ar, 1)
            dve.tensor_copy(wo_hi[:, :, :], wo_f[:, :, :])
            after(dve, dve.tensor_copy(wq_hi[:, 0, :], wq_f[:, 0, :]))
            dve.tensor_tensor(wo_lo[:, :, :], wo_f[:, :, :], wo_hi[:, :, :].bitcast(F32), ALU.subtract)
            dve.tensor_tensor(wq_lo[:, 0, :], wq_f[:, 0, :], wq_hi[:, 0, :].bitcast(F32), ALU.subtract)
            add_row(dve, 2, 0)
            lg, ex, pr, rank, w = (moe[:, i, :].rearrange("p (t e) -> p t e", e=NE) for i in range(5))
            mx, sm, rc = (moe[:, 5 + i, 0:NT] for i in range(3))
            gt, eq = (ksq[:, i, 0:NT * NE * NE].rearrange("p (t e f) -> p t e f", e=NE, f=NE) for i in range(2))
            gt3, eq3 = (z.rearrange("p t e f -> p t (e f)") for z in (gt, eq))

            def wide(z):
                return z.unsqueeze(2).broadcast_to([P, NT, NE])

            for t in range(NT):
                dve.wait_ge(f2_h, t + 1)
                ins = dve.tensor_copy(lg[:, t, :], f2_h_banks[t][:, NE * RANK:AR])
            after(dve, ins)
            after(dve, dve.tensor_reduce(mx, lg, AX.X, ALU.max))
            dve.tensor_tensor(lg, lg, wide(mx), ALU.subtract).then_inc(f2_lg, 1)
            dve.wait_ge(f2_exp, 1)
            after(dve, dve.tensor_reduce(sm, ex, AX.X, ALU.add))
            after(dve, dve.reciprocal(rc, sm))
            after(dve, dve.tensor_tensor(pr, ex, wide(rc), ALU.mult))
            pf = pr.unsqueeze(2).broadcast_to([P, NT, NE, NE])
            pe_ = pr.unsqueeze(3).broadcast_to([P, NT, NE, NE])
            dve.tensor_tensor(gt, pf, pe_, ALU.is_gt)
            after(dve, dve.tensor_tensor(eq, pf, pe_, ALU.is_equal))
            before = vecs[:, 0:NE * NE].unsqueeze(1).broadcast_to([P, NT, NE * NE])
            after(dve, dve.tensor_tensor(eq3, eq3, before, ALU.mult))
            after(dve, dve.tensor_tensor(gt3, gt3, eq3, ALU.add))
            after(dve, dve.tensor_reduce(rank, gt, AX.X, ALU.add))
            after(dve, dve.scalar_tensor_tensor(w, rank, 2.0, pr, ALU.is_lt, ALU.mult))
            after(dve, dve.tensor_reduce(sm, w, AX.X, ALU.add))
            after(dve, dve.reciprocal(rc, sm))
            after(dve, dve.scalar_tensor_tensor(w, w, 2.0, wide(rc), ALU.mult, ALU.mult))
            for t in range(NT):
                hw = flat(scr[:, :, :])[:, t * P:(t + 1) * P].rearrange("p (e r) -> p e r", r=RANK)
                ins = dve.tensor_tensor(hw, f2_h_banks[t][:, 0:NE * RANK].rearrange("p (e r) -> p e r", r=RANK),
                                        w[:, t, :].unsqueeze(2).broadcast_to([P, NE, RANK]), ALU.mult)
            ins.then_inc(f2_hw, 1)
            dve.wait_ge(f2_hwhi, 1)
            dve.tensor_tensor(q_lo[:, 0, :], psO[:, :], q_hi[:, 0, :].bitcast(F32), ALU.subtract).then_inc(f2_hwlo, 1)
            add_tiles(dve, 2, f2_out_banks, f2_out)

        def f2_scalar(act):
            act.wait_ge(f2_lg, 1)
            act.activation(moe[:, 1, :], moe[:, 0, :], ACT.Exp).then_inc(f2_exp, 1)
            act.wait_ge(f2_tp, 1)
            act.activation(q_hi[:, 0, :], psO[:, :], ACT.Copy).then_inc(f2_hwhi, 1)

        f3_ab_banks = [psX[:, 0, :], psX[:, 1, :], psO[:, :], psQ[:, :]]
        f3_out_banks = ln_banks

        def f3_sync(sp):
            sp.wait_ge(x_ready, 8)
            sp.dma_start(wo_f[:, :, :], a["f3_wT"]).then_inc(f3_dma, 16)
            sp.dma_start(wq_f[0:RANK, 0, :], a["L3_ffn_B"]).then_inc(f3_dma, 16)
            sp.dma_start(wq_f[0:RANK, 1, :], a["f3_aT"]).then_inc(f3_dma, 16)
            sp.dma_start(rows[:, :], a["L3_ffn_bias"].partition_broadcast(P)).then_inc(f3_dma, 16)

        def f3_tensor(pe):
            pe.wait_ge(f3_dma, 64)
            for c in range(DC):
                pe.matmul(f3_ab_banks[c], wq_f[0:RANK, 0, c * P:(c + 1) * P], wq_f[0:RANK, 1, :],
                          start=True, stop=True).then_inc(f3_ab, 1)

        def f3_tensor_out(pe):
            pe.wait_ge(f3_w, 1)
            for t in range(NT):
                pe.wait_ge(ln_lo, 7 * NT + t + 1)
                three(pe, f3_out_banks[t], [(xn_tile(t, c), [z[:, c, :] for z in (wo_hi, wo_lo)])
                                            for c in range(DC)]).then_inc(f3_out, 1)

        def f3_vector(dve):
            dve.wait_ge(f3_dma, 64)
            add_row(dve, 3, 0)
            for c in range(DC):
                dve.wait_ge(f3_ab, c + 1)
                ins = dve.scalar_tensor_tensor(wo_f[:, c, :], f3_ab_banks[c], 1.0 / RANK, wo_f[:, c, :],
                                               ALU.mult, ALU.add)
            after(dve, ins)
            after(dve, dve.tensor_copy(wo_hi[:, :, :], wo_f[:, :, :]))
            dve.tensor_tensor(wo_lo[:, :, :], wo_f[:, :, :], wo_hi[:, :, :].bitcast(F32), ALU.subtract).then_inc(f3_w, 1)
            add_tiles(dve, 3, f3_out_banks, f3_out)

        block = ctx.enter_context(nc.Block())

        @block.sync
        def _(sp):
            start_sync(sp)
            for L, ffn in zip(layers, (f0_sync, f1_sync, f2_sync, f3_sync)):
                attn_sync(sp, L)
                ffn(sp)
            sp.wait_ge(x_ready, 9)
            sp.dma_start(out.rearrange("b (t p) d -> p (b t) d", p=P), x_sb[:, :, :]).then_inc(out_dma, 16)
            sp.wait_ge(out_dma, 16)

        @block.tensor
        def _(pe):
            for L, ffn in zip(layers, (f0_tensor, f1_tensor, f2_tensor, f3_tensor_out)):
                ln_tensor(pe, 2 * L.i)
                pe.wait_ge(ln_lo, NT * (2 * L.i + 1))
                attn_tensor(pe, L)
                ln_tensor(pe, 2 * L.i + 1)
                if L.i == 3:
                    f3_tensor(pe)
                ffn(pe)

        @block.vector
        def _(dve):
            start_vector(dve)
            dve.wait_ge(const_dma, 48)
            finish(dve, 0, lambda t: None)
            for L, ffn in zip(layers, (f0_vector, f1_vector, f2_vector, f3_vector)):
                attn_vector(dve, L)
                ffn(dve)

        @block.scalar
        def _(act):
            start_scalar(act)
            for L, ffn in zip(layers, (f0_scalar, f1_scalar, f2_scalar, lambda act: None)):
                ln_scalar(act, 2 * L.i)
                attn_scalar(act, L)
                ln_scalar(act, 2 * L.i + 1)
                ffn(act)

        @block.gpsimd
        def _(pool):
            for L, ffn in zip(layers, (f0_gpsimd, f1_gpsimd, lambda pool: None, lambda pool: None)):
                ln_gpsimd(pool, 2 * L.i)
                attn_gpsimd(pool, L)
                ln_gpsimd(pool, 2 * L.i + 1)
                ffn(pool)


def kernel(**inputs):
    import numpy as np
    import concourse.bacc as bacc
    from concourse.bass_utils import run_bass_kernel_spmd

    z = {k: np.asarray(v) for k, v in inputs.items()}

    def split(w, parts):
        d, n = w.shape
        return w.reshape(d // P, P, parts, n // parts).transpose(2, 1, 0, 3)

    def cols(w):
        return w.reshape(DC, P, -1).transpose(1, 0, 2)

    def attn(i, wq, wk, wv, wo, n, hd):
        arrays[f"a{i}_wq"] = split(wq, n * G4).reshape(n * G4, P, DC * hd)
        k, v = (split(w, n).reshape(n, P, DC * hd) for w in (wk, wv))
        arrays[f"a{i}_wkv"] = np.stack([k, v], axis=2)
        arrays[f"a{i}_wo"] = wo.reshape(n, G4, hd, D).transpose(0, 2, 1, 3)

    arrays = {"x": z["x"], "ctxT": cols(z["ctx_4096"].reshape(B * CTX, D).T),
              "g_xattn": z["g_xattn"], "g_ffn": z["g_ffn"]}
    arrays["c_ident"] = np.eye(P, dtype=np.float32)
    arrays["c_ones"] = np.ones((P, P), np.float32)
    hd = 128
    inv_freq = (np.float32(1.0) / np.float32(10000.0) ** (np.arange(0, hd, 2, dtype=np.float32) / np.float32(hd))).astype(np.float32)
    ang = (np.arange(SQ, dtype=np.float32)[:, None] * inv_freq[None, :]).astype(np.float32)
    cos, sin = np.cos(ang).T, np.sin(ang).T
    cos, sin = np.concatenate([cos, cos]), np.concatenate([sin, -sin])
    causal = np.where(np.arange(SQ)[:, None] >= np.arange(SQ)[None, :], 0.0, NEG).astype(np.float32)
    arrays["c_causal_trig"] = np.concatenate([causal.reshape(2, P, SQ).transpose(1, 0, 2).reshape(P, 2 * SQ), cos, sin],
                                             axis=1).astype(np.float32)
    arrays["c_before"] = (np.arange(NE)[None, :] < np.arange(NE)[:, None]).astype(np.float32).reshape(-1)

    wkv = z["L0_xattn_Wkv"]
    attn(0, z["L0_xattn_Wq"], wkv[:, :1024], wkv[:, 1024:], z["L0_xattn_Wo"], 8, 128)
    attn(1, z["L1_xattn_Wq"].T, z["L1_xattn_Wk"].T, z["L1_xattn_Wv"].T, z["L1_xattn_Wd"].T, 8, 128)
    attn(2, z["L2_xattn_Wq"].T, z["L2_xattn_Wk"].T, z["L2_xattn_Wv"].T, z["L2_xattn_Wo"].T, 4, 96)
    attn(3, z["L3_xattn_Wq"].T, z["L3_xattn_Wk"].T, z["L3_xattn_Wv"].T, z["L3_xattn_Wo"].T, 8, 128)
    arrays["a0_vecs"] = np.concatenate([z["L0_xattn_bq"].reshape(32, P), z["L0_xattn_bkv"].reshape(16, P)]).T
    arrays["a3_vecs"] = np.stack([z["L3_xattn_q_norm_w"], z["L3_xattn_k_norm_w"]], axis=1)
    arrays["a3_mask"] = z["mask_1x1xSxS2_ff0"].reshape(2, P, CTX).transpose(1, 0, 2).reshape(P, 2 * CTX)
    arrays["L0_xattn_bo"] = z["L0_xattn_bo"]
    arrays["f0_wT"] = cols(z["L0_ffn_weight"].T)
    for k in ("bias", "scale", "ln_gamma", "ln_beta", "quant_scale"):
        arrays[f"L0_ffn_{k}"] = z[f"L0_ffn_{k}"]

    def chunks(up, down):
        up, down = up.reshape(H1, D).T.reshape(DC, P, H1), down.reshape(D, H1).T
        parts = []
        for c in range(0, H1, P):
            n = min(P, H1 - c)
            parts.append(up[:, :, c:c + n].transpose(1, 0, 2).reshape(P, DC * n))
            parts.append(np.concatenate([down[c:c + n], np.zeros((P - n, D), down.dtype)]))
        return np.concatenate(parts, axis=1)

    arrays["codes"] = chunks(z["L1_ffn_w_up_codes"], z["L1_ffn_w_down_codes"])
    arrays["amax"] = chunks(*(np.repeat(z[f"L1_ffn_w_{k}_absmax"], 64) for k in ("up", "down")))
    down_a = np.concatenate([z["L1_ffn_w_down_lora_a"], np.zeros((H1C * P - H1, RANK), np.float32)])
    arrays["f1_la"] = np.concatenate([cols(z["L1_ffn_w_up_lora_a"]).reshape(P, -1),
                                      down_a.reshape(H1C, P, RANK).transpose(1, 0, 2).reshape(P, -1)], axis=1)
    arrays["f1_lb"] = np.concatenate([z["L1_ffn_w_up_lora_b"], z["L1_ffn_w_down_lora_b"]], axis=1)
    arrays["f1_b_up"] = np.concatenate([z["L1_ffn_b_up"], np.zeros(H1C * P - H1, np.float32)]).reshape(H1C, P).T
    arrays["L1_ffn_b_down"] = z["L1_ffn_b_down"]
    arrays["f2_ar"] = cols(np.concatenate([z["L2_ffn_A"].reshape(NE * RANK, D), z["L2_ffn_W_router"]]).T).reshape(P, -1)
    arrays["f2_wT"] = cols(z["L2_ffn_W_base"].T)
    arrays["f2_b"] = z["L2_ffn_B"].transpose(0, 2, 1).reshape(NE * RANK, D)
    arrays["L2_ffn_b_base"] = z["L2_ffn_b_base"]
    arrays["f3_wT"] = cols(z["L3_ffn_W_q"].T)
    arrays["L3_ffn_B"] = z["L3_ffn_B"]
    arrays["f3_aT"] = z["L3_ffn_A"].T
    arrays["L3_ffn_bias"] = z["L3_ffn_bias"]

    nc = bacc.Bacc("TRN2", target_bir_lowering=False, num_devices=1, dynamic_dma_scratch_size=1024)
    a, feed = {}, {}
    for name, v in arrays.items():
        v = np.ascontiguousarray(v)
        feed["in_" + name] = v
        a[name] = nc.dram_tensor("in_" + name, v.shape, mybir.dt.from_np(v.dtype), kind="ExternalInput").ap()
    for i in range(4):
        a[f"attn{i}"] = {k: a[f"a{i}_{k}"] for k in ("wq", "wkv", "wo", "vecs", "mask") if f"a{i}_{k}" in a}
    a["attn1"]["mask"] = a["c_causal_trig"]
    out = nc.dram_tensor("out", (B, SQ, D), F32, kind="ExternalOutput").ap()
    scratch = nc.dram_tensor("w1", (P, W1_COLS), F32).ap()
    program(nc, a, out, scratch)
    r = run_bass_kernel_spmd(nc, [feed], core_ids=[0])
    return r.results[0]["out"]
```
